# Optimizing a Trainium2 kernel written in Bass

```python
import numpy as np
import jax
import jax.numpy as jnp

def _softmax(x, axis=-1):
    return jax.nn.softmax(x, axis=axis)

def _gelu(x):
    return jax.nn.gelu(x, approximate=True)

def _silu(x):
    return jax.nn.silu(x)

def _sigmoid(x):
    return jax.nn.sigmoid(x)

def _layernorm(x, axis=-1, eps=1e-05):
    m = jnp.mean(x, axis=axis, keepdims=True)
    v = jnp.var(x, axis=axis, keepdims=True)
    return (x - m) / jnp.sqrt(v + eps)

def _scatter_add(tgt, idx, src, axis=0):
    return tgt.at[idx].add(src)

def _segment_sum(src, seg, n):
    return jax.ops.segment_sum(src, seg, n)
kernel_name = 'mk_adaln_ffn_d2_seqx_r8_3965dc'

def setup_inputs(seed: int=0):
    np.random.seed(seed)
    _w = jnp.asarray

    def _rec_inputs():
        import jax
        import jax.numpy as jnp
        _rk = jax.random.key(seed)
        x = -0.0002071 + 1 * jax.random.normal(jax.random.fold_in(_rk, 1), (8, 128, 128), jnp.float32)
        _lenS = 128 - jax.random.randint(jax.random.fold_in(_rk, 7), (8,), 0, max(1, 128 // 4) + 1, jnp.int32)
        _lenS2 = 128 - jax.random.randint(jax.random.fold_in(_rk, 8), (8,), 0, max(1, 128 // 4) + 1, jnp.int32)
        cond_8 = jax.random.uniform(jax.random.fold_in(_rk, 11), (8, 8), jnp.float32, 0.0, 0.983423)
        return (x, cond_8)
    x, cond_8 = _rec_inputs()

    def _L0_cond_setup():
        import jax, jax.numpy as jnp
        import numpy as np
        R = 16
        ALPHA = 32.0
        SCALING = ALPHA / R
        key = jax.random.key(seed)
        ks = jax.random.split(key, 6)
        B, T, C, O, E = (16, 1500, 128, 128, 8)
        x = jax.random.normal(ks[0], (B, T, C), dtype=jnp.float32)
        w = jax.random.uniform(ks[1], (B, E), dtype=jnp.float32)
        W_base = jax.random.normal(ks[2], (O, C), dtype=jnp.float32) * 0.02
        b_base = jax.random.normal(ks[3], (O,), dtype=jnp.float32) * 0.02
        As = jax.random.normal(ks[4], (E, R, C), dtype=jnp.float32) * 0.02
        Bs = jax.random.normal(ks[5], (E, O, R), dtype=jnp.float32) * 0.02
        return {'x': x, 'w': w, 'W_base': W_base, 'b_base': b_base, 'As': As, 'Bs': Bs}
    _L0_cond_all = _L0_cond_setup()
    _L0_cond_in = {k: v for k, v in _L0_cond_all.items() if k in ('W_base', 'b_base', 'As', 'Bs')}
    del _L0_cond_all

    def _L0_ffn_setup():
        import jax, jax.numpy as jnp
        import numpy as np
        B, N, C, F, E, K = (2, 256, 128, 512, 8, 2)
        key = jax.random.key(seed)
        k = jax.random.split(key, 6)
        xavier1 = float(np.sqrt(6.0 / (C + F)))
        xavier2 = float(np.sqrt(6.0 / (F + C)))
        return {'x': jax.random.normal(k[0], (B, N, C), dtype=jnp.float32), 'router_w': jax.random.normal(k[1], (E, C), dtype=jnp.float32) * 0.01, 'w1': jax.random.uniform(k[2], (E, F, C), dtype=jnp.float32, minval=-xavier1, maxval=xavier1), 'b1': jnp.zeros((E, F), dtype=jnp.float32), 'w2': jax.random.uniform(k[3], (E, C, F), dtype=jnp.float32, minval=-xavier2, maxval=xavier2), 'b2': jnp.zeros((E, C), dtype=jnp.float32)}
    _L0_ffn_all = _L0_ffn_setup()
    _L0_ffn_in = {k: v for k, v in _L0_ffn_all.items() if k in ('router_w', 'w1', 'b1', 'w2', 'b2')}
    del _L0_ffn_all

    def _L1_cond_setup():
        import jax, jax.numpy as jnp
        import numpy as np
        B, S, D = (16, 256, 128)
        E, H = (8, 256)
        key = jax.random.key(seed)
        ks = jax.random.split(key, 8)
        scale = 0.02
        x = jax.random.normal(ks[0], (B, S, D), dtype=jnp.float32)
        opcode_onehot = jax.random.uniform(ks[1], (B, E), dtype=jnp.float32)
        W_up = jax.random.normal(ks[2], (E, H, D), dtype=jnp.float32) * scale
        b_up = jnp.zeros((E, H), dtype=jnp.float32)
        W_gate = jax.random.normal(ks[3], (E, H, D), dtype=jnp.float32) * scale
        b_gate = jnp.zeros((E, H), dtype=jnp.float32)
        W_down = jax.random.normal(ks[4], (E, D, H), dtype=jnp.float32) * scale
        b_down = jnp.zeros((E, D), dtype=jnp.float32)
        return {'x': x, 'opcode_onehot': opcode_onehot, 'W_up': W_up, 'b_up': b_up, 'W_gate': W_gate, 'b_gate': b_gate, 'W_down': W_down, 'b_down': b_down}
    _L1_cond_all = _L1_cond_setup()
    _L1_cond_in = {k: v for k, v in _L1_cond_all.items() if k in ('W_up', 'b_up', 'W_gate', 'b_gate', 'W_down', 'b_down')}
    del _L1_cond_all

    def _L1_ffn_setup():
        import jax, jax.numpy as jnp
        import numpy as np
        B, L, H, E, FF, C = (4, 256, 128, 8, 512, 2)
        key = jax.random.key(seed)
        ks = jax.random.split(key, 6)
        s = 0.02
        return {'x': jax.random.normal(ks[0], (B, L, H), dtype=jnp.float32), 'Wg': jax.random.normal(ks[1], (H, E), dtype=jnp.float32) * s, 'W1': jax.random.normal(ks[2], (E, H, FF), dtype=jnp.float32) * s, 'b1': jnp.zeros((E, FF), dtype=jnp.float32), 'W2': jax.random.normal(ks[3], (E, FF, H), dtype=jnp.float32) * s, 'b2': jnp.zeros((E, H), dtype=jnp.float32)}
    _L1_ffn_all = _L1_ffn_setup()
    _L1_ffn_in = {k: v for k, v in _L1_ffn_all.items() if k in ('Wg', 'W1', 'b1', 'W2', 'b2')}
    del _L1_ffn_all
    return {'x': x, 'cond_8': cond_8, 'L0_cond_W_base': _L0_cond_in['W_base'], 'L0_cond_b_base': _L0_cond_in['b_base'], 'L0_cond_As': _L0_cond_in['As'], 'L0_cond_Bs': _L0_cond_in['Bs'], 'L0_ffn_router_w': _L0_ffn_in['router_w'], 'L0_ffn_w1': _L0_ffn_in['w1'], 'L0_ffn_b1': _L0_ffn_in['b1'], 'L0_ffn_w2': _L0_ffn_in['w2'], 'L0_ffn_b2': _L0_ffn_in['b2'], 'L1_cond_W_up': _L1_cond_in['W_up'], 'L1_cond_b_up': _L1_cond_in['b_up'], 'L1_cond_W_gate': _L1_cond_in['W_gate'], 'L1_cond_b_gate': _L1_cond_in['b_gate'], 'L1_cond_W_down': _L1_cond_in['W_down'], 'L1_cond_b_down': _L1_cond_in['b_down'], 'L1_ffn_Wg': _L1_ffn_in['Wg'], 'L1_ffn_W1': _L1_ffn_in['W1'], 'L1_ffn_b1': _L1_ffn_in['b1'], 'L1_ffn_W2': _L1_ffn_in['W2'], 'L1_ffn_b2': _L1_ffn_in['b2']}

def reference(x, cond_8, L0_cond_W_base, L0_cond_b_base, L0_cond_As, L0_cond_Bs, L0_ffn_router_w, L0_ffn_w1, L0_ffn_b1, L0_ffn_w2, L0_ffn_b2, L1_cond_W_up, L1_cond_b_up, L1_cond_W_gate, L1_cond_b_gate, L1_cond_W_down, L1_cond_b_down, L1_ffn_Wg, L1_ffn_W1, L1_ffn_b1, L1_ffn_W2, L1_ffn_b2):
    import jax
    import jax.numpy as jnp

    def _L0_cond_ref(x, w, W_base, b_base, As, Bs):
        import jax, jax.numpy as jnp
        import numpy as np
        R = 16
        ALPHA = 32.0
        SCALING = ALPHA / R
        out = jnp.einsum('btc,oc->bto', x, W_base) + b_base
        h = jnp.einsum('btc,erc->bter', x, As)
        lora = jnp.einsum('bter,eor,be->bto', h, Bs, w)
        return out + lora * SCALING

    def _L0_ffn_ref(x, router_w, w1, b1, w2, b2):
        import jax, jax.numpy as jnp
        import numpy as np
        B, N, C, F, E, K = (2, 256, 128, 512, 8, 2)
        Bb, Nn, Cc = x.shape
        x_flat = x.reshape(-1, Cc)
        logits = jnp.einsum('tc,ec->te', x_flat, router_w)
        probs = jax.nn.softmax(logits, axis=-1)
        top_w, top_idx = jax.lax.top_k(probs, K)
        top_w = top_w / (jnp.sum(top_w, axis=-1, keepdims=True) + 1e-09)
        h = jnp.einsum('tc,efc->tef', x_flat, w1) + b1[None]
        h = jax.nn.relu(h)
        y = jnp.einsum('tef,ecf->tec', h, w2) + b2[None]
        sel = jnp.take_along_axis(y, top_idx[:, :, None], axis=1)
        out = jnp.einsum('tkc,tk->tc', sel, top_w)
        return out.reshape(Bb, Nn, Cc)

    def _L1_cond_ref(x, opcode_onehot, W_up, b_up, W_gate, b_gate, W_down, b_down):
        import jax, jax.numpy as jnp
        import numpy as np
        B, S, D = (16, 256, 128)
        E, H = (8, 256)
        expert = jnp.argmax(opcode_onehot, axis=-1)
        wu, bu = (W_up[expert], b_up[expert])
        wg, bg = (W_gate[expert], b_gate[expert])
        wd, bd = (W_down[expert], b_down[expert])
        up = jnp.einsum('bsd,bhd->bsh', x, wu) + bu[:, None, :]
        gate = jnp.einsum('bsd,bhd->bsh', x, wg) + bg[:, None, :]
        hidden = jax.nn.silu(up) * gate
        out = jnp.einsum('bsh,bdh->bsd', hidden, wd) + bd[:, None, :]
        return out

    def _L1_ffn_ref(x, Wg, W1, b1, W2, b2):
        import jax, jax.numpy as jnp
        import numpy as np
        B, L, H, E, FF, C = (4, 256, 128, 8, 512, 2)
        b, l, h = x.shape
        e = Wg.shape[1]
        n = b * l
        k = min(max(int(n * C / e), 1), n)
        xt = x.reshape(n, h)
        S = jax.nn.sigmoid(xt @ Wg).T
        G, I = jax.lax.top_k(S, k)
        ex = xt[I]
        hid = jax.nn.gelu(jnp.einsum('ekh,ehf->ekf', ex, W1) + b1[:, None, :], approximate=False)
        out = (jnp.einsum('ekf,efh->ekh', hid, W2) + b2[:, None, :]) * G[..., None]
        new_x = jnp.zeros_like(xt).at[I.reshape(-1)].add(out.reshape(-1, h))
        return new_x.reshape(b, l, h)
    x = x + _L0_ffn_ref(_L0_cond_ref(x, cond_8, L0_cond_W_base, L0_cond_b_base, L0_cond_As, L0_cond_Bs), L0_ffn_router_w, L0_ffn_w1, L0_ffn_b1, L0_ffn_w2, L0_ffn_b2)
    x = x + _L1_ffn_ref(_L1_cond_ref(x, cond_8, L1_cond_W_up, L1_cond_b_up, L1_cond_W_gate, L1_cond_b_gate, L1_cond_W_down, L1_cond_b_down), L1_ffn_Wg, L1_ffn_W1, L1_ffn_b1, L1_ffn_W2, L1_ffn_b2)
    return x

_drawn_inputs = setup_inputs


def setup_inputs(seed=0):
    import zlib

    import numpy as np

    out = dict(_drawn_inputs(seed))
    spreads = {'L0_ffn_b1': (0.0, 0.1),
     'L0_ffn_b2': (0.0, 0.1),
     'L1_cond_b_up': (0.0, 0.296),
     'L1_cond_b_gate': (0.0, 0.301),
     'L1_cond_b_down': (0.0, 0.1),
     'L1_ffn_b1': (0.0, 0.485),
     'L1_ffn_b2': (0.0, 0.1)}
    factors = {'L1_ffn_W1': 8.0, 'L1_ffn_W2': 3.544}
    for name, (base, spread) in spreads.items():
        noise = np.random.default_rng([zlib.crc32(name.encode()), seed]).standard_normal(out[name].shape)
        drawn = base * np.exp(spread * noise) if base else spread * noise
        out[name] = jnp.asarray(drawn.astype(out[name].dtype))
    for name, factor in factors.items():
        out[name] = (out[name] * factor).astype(out[name].dtype)
    return out
```

```python
from contextlib import ExitStack

import numpy as np

import concourse.bass as bass
from concourse import mybir

P = 128
T, C = 1024, 128
NC = T // P
E = 8
R = 16
F = 512
NF = F // P
H = 256
K = 2
LORA_SCALE = 32.0 / R
NB = K * T // P + E - 1
NBP = NB + 1
CAP = 256
NH = CAP // P
PAD = 4096
ROW = C + E
DIGIT = 3
STEPS = 30 // DIGIT
NJ = 2 ** DIGIT - 1
NEG = -3.0e38

F32 = mybir.dt.float32
BF16 = mybir.dt.bfloat16
I32 = mybir.dt.int32
ALU = mybir.AluOpType
ACT = mybir.ActivationFunctionType
AX = mybir.AxisListType

_WIDTHS = [("ident", P), ("tri", P), ("iota", P), ("rev", E), ("pcol", 1), ("blk0", E), ("lt", E * E),
           ("dval", K * NC), ("cval", NC)]
_AT, _n = {}, 0
for _name, _w in _WIDTHS:
    _AT[_name] = (_n, _n + _w)
    _n += _w
CONSTS = _n
WU, WG, WD, BU, BG, BD = 0, H, 2 * H, 3 * H, 3 * H + 2, 3 * H + 4
CW = 3 * H + 5


def constants():
    t = np.zeros((P, CONSTS), np.float32)
    p = np.arange(P)

    def put(name, v):
        a, b = _AT[name]
        t[:, a:b] = v

    put("ident", np.eye(P))
    put("tri", p[:, None] < p[None, :])
    put("iota", p[None, :])
    put("rev", E - np.arange(E)[None, :])
    put("pcol", p[:, None])
    put("blk0", P * np.arange(E)[None, :])
    e = np.arange(E)
    put("lt", (e[None, :] < e[:, None]).reshape(1, -1))
    k, c = np.meshgrid(np.arange(K), np.arange(NC), indexing="ij")
    put("dval", (P * c + T * k - PAD).reshape(1, -1))
    put("cval", P * np.arange(NC)[None, :])
    shifts = DIGIT * np.arange(STEPS - 1, -1, -1)
    digits = (np.arange(1, NJ + 1)[None, :] << shifts[:, None]).astype(np.int32)
    return t, digits.reshape(1, -1), (2.0 ** shifts).astype(np.float32).reshape(1, -1)


def adaln_moe(nc, xT, x, lora_a, lora_b, w_base, b_base, cond_rep, cond_row, router, w1, b1, w2, b2,
              cond_w, gate_w, v1, c1, v2, c2b, consts, digits, powers, out):
    with ExitStack() as ctx:
        def sb(name, shape, dt=F32):
            return ctx.enter_context(nc.sbuf_tensor(name, shape, dt))

        def sem(name):
            return ctx.enter_context(nc.semaphore(name))

        rows0 = nc.dram_tensor("rows0", (T, C), F32).ap()
        rows1 = nc.dram_tensor("rows1", (T, ROW), F32).ap()
        picked = nc.dram_tensor("picked", (K * T, C), F32).ap()

        bank = [ctx.enter_context(nc.psum_tensor(f"bank{i}", [P, 512], F32)) for i in range(8)]

        xT_sb = sb("xT_sb", [P, T])
        x_sb = sb("x_sb", [P, NC, C])
        a_sb = sb("a_sb", [P, E * R])
        b_sb = sb("b_sb", [P, C])
        wb_sb = sb("wb_sb", [P, C])
        bb_sb = sb("bb_sb", [P, 1])
        cr_sb = sb("cr_sb", [P, NC])
        crow = sb("crow", [1, NC, E])
        rt_sb = sb("rt_sb", [P, E])
        w1_sb = sb("w1_sb", [P, E * F])
        b1_sb = sb("b1_sb", [P, E * F])
        w2_sb = sb("w2_sb", [P, E * NF * C])
        b2_sb = sb("b2_sb", [P, E * C])
        cw_sb = sb("cw_sb", [P, NC, CW])
        gw_sb = sb("gw_sb", [P, E])
        v1_sb = sb("v1_sb", [P, E, F])
        c1_sb = sb("c1_sb", [P, E * NF])
        v2_sb = sb("v2_sb", [P, E, NF, C])
        c2b_sb = sb("c2b_sb", [P, E, C])
        cst = sb("cst", [P, CONSTS])
        dig_sb = sb("dig_sb", [P, STEPS * NJ], I32)
        pow_sb = sb("pow_sb", [P, STEPS])

        def const(name):
            a, b = _AT[name]
            return cst[:, a:b]

        tri = sb("tri", [P, P], BF16)
        iota = sb("iota", [P, P], BF16)
        ones = sb("ones", [P, P], BF16)

        cr2 = sb("cr2", [P, NC])
        hs = sb("hs", [P, T])
        cT = sb("cT", [P, T])
        c_tok = sb("c_tok", [P, NC, C])
        lg = sb("lg", [P, NC, E])
        lg2 = sb("lg2", [P, NC, E])
        eq = sb("eq", [P, NC, E])
        top = sb("top", [P, K, NC])
        mr = sb("mr", [P, NC])
        sel = sb("sel", [P, K, NC, E])
        mask = sb("mask", [P, NC, E], BF16)
        nbig = sb("nbig", [P, E, E])
        nblk = sb("nblk", [P, E])
        before = sb("before", [P, E, E])
        cblk = sb("cblk", [P, E])
        cinc = sb("cinc", [P, E])
        base = sb("base", [P, E])
        pos = sb("pos", [P, NC, E])
        psel = sb("psel", [P, K, NC, E])
        posk = sb("posk", [P, K * NC], I32)
        blk = sb("blk", [P, K * NC], I32)
        loc = sb("loc", [P, K * NC], I32)
        slot1h = sb("slot1h", [P, K * NC, P], BF16)
        blk1h = sb("blk1h", [P, K * NC, NBP], BF16)
        blkv = sb("blkv", [P, K * NC, 2, NBP], BF16)
        idxf = sb("idxf", [P, NBP])
        sidx = sb("sidx", [P, NBP], I32)
        gidx = sb("gidx", [P, NBP], I32)
        bexp = sb("bexp", [1, NBP, E])
        bexf = sb("bexf", [1, NBP])
        bexi = sb("bexi", [1, NBP], I32)
        shifted = sb("shifted", [P, NC, E])
        expd = sb("expd", [P, NC, E])
        zsum = sb("zsum", [P, NC])
        dif2 = sb("dif2", [P, NC])
        wt = sb("wt", [P, K, NC])
        den = sb("den", [P, NC])
        den2 = sb("den2", [P, NC])

        xs = sb("xs", [P, 2, C])
        xsT = sb("xsT", [P, 2, P])
        hb = sb("hb", [P, 2, F])
        hT = sb("hT", [P, 2, F])
        y0 = sb("y0", [P, NBP, C])
        got = b1_sb[:, 0:K * NC * C].rearrange("p (k c d) -> p k c d", k=K, c=NC)
        xa = hs[:].rearrange("p (c d) -> p c d", c=NC)
        x1 = sb("x1", [P, NC, C])

        carg = sb("carg", [1, NC, E])
        cmax = sb("cmax", [1, NC])
        cexp = sb("cexp", [1, NC], I32)
        x1T = sb("x1T", [P, 2, P])
        su = sb("su", [P, 2, 2, P])
        hid = sb("hid", [P, 2, 2, P])
        dT = sb("dT", [P, T])
        row = sb("row", [P, NC, ROW])
        th = sb("th", [P, NC, E])
        sc = sb("sc", [P, NC, E])
        tau = sb("tau", [P, E], I32)
        thr = sb("thr", [P, E, NJ], I32)
        cmp_ = sb("cmp", [P, NC, E * NJ], BF16)
        flag = sb("flag", [P, E, NJ])
        inc = sb("inc", [P, E], I32)
        gteq = sb("gteq", [P, 2, NC * E], BF16)
        ngt = sb("ngt", [P, E])
        pe_ = sb("pe_", [P, NC, E])
        pg_ = sb("pg_", [P, NC, E])
        pos1 = sb("pos1", [P, NC, E])
        posi = sb("posi", [P, NC * E], I32)
        half = sb("half", [P, NC * E], I32)
        loc1 = sb("loc1", [P, NC * E], I32)
        one1 = slot1h[:].rearrange("p (r c) s -> p r c s", r=2)
        hlf1h = sb("hlf1h", [P, NC * E, NH], BF16)
        hlfv = sb("hlfv", [P, NC, E, 2, NH], BF16)
        idx1 = sb("idx1", [P, E * NH], I32)
        xg = sb("xg", [P, E * NH, ROW])
        xgT = sb("xgT", [P, 2, CAP])
        h1T = b1_sb[:, K * NC * C:].rearrange("p (r f s) -> p r f s", r=2, f=NF)
        yb = sb("yb", [P, 2, NH, C])
        y1 = sb("y1", [P, 2, NH, C])

        in_cond, in_const, in_w1, in_w2, in_x, in_cw = (sem(n) for n in (
            "in_cond", "in_const", "in_w1", "in_w2", "in_x", "in_cw"))
        in_gw, in_v = sem("in_gw"), sem("in_v")
        dve = sem("dve_steps")
        consts_ready = sem("consts_ready")
        cexp_ready = sem("cexp_ready")
        lora_h, lora_s, proj, cT_ready, logits = (sem(n) for n in (
            "lora_h", "lora_s", "proj", "cT_ready", "logits"))
        c_turned, c_tok_ready, rows0_written = sem("c_turned"), sem("c_tok_ready"), sem("rows0_written")
        mask_ready, prefix, onehots, slots = (sem(n) for n in ("mask_ready", "prefix", "onehots", "slots"))
        idx_ready, bexp_ready, shift_ready, exp_ready = (sem(n) for n in (
            "idx_ready", "bexp_ready", "shift_ready", "exp_ready"))
        gathered = [sem("gathered_even"), sem("gathered_odd")]
        x_turned, xsT_ready, h_ready, hb_ready, h_turned, hT_ready, y_ready, y_kept, scattered, got_in = (
            sem(n) for n in ("x_turned", "xsT_ready", "h_ready", "hb_ready", "h_turned", "hT_ready",
                             "y_ready", "y_kept", "scattered", "got_in"))
        x1_ready, x1_turned, x1T_ready, upgate, silu_ready, hid_ready, down, dT_ready = (sem(n) for n in (
            "x1_ready", "x1_turned", "x1T_ready", "upgate", "silu_ready", "hid_ready", "down", "dT_ready"))
        d_turned, row_ready, logits1, tanh_ready, sc_ready, rows1_written, out_init = (sem(n) for n in (
            "d_turned", "row_ready", "logits1", "tanh_ready", "sc_ready", "rows1_written", "out_init"))
        cmp_ready, counted, gteq_ready, prefix1, onehot1, slots1, idx1_ready = (sem(n) for n in (
            "cmp_ready", "counted", "gteq_ready", "prefix1", "onehot1", "slots1", "idx1_ready"))
        gathered1 = [sem(f"gathered1_{e}") for e in range(E)]
        added = [sem(f"added_{e}") for e in range(E)]
        xg_turned, xgT_ready, h1_ready, h1T_ready, y1_ready, y1_kept, y1_sent = (sem(n) for n in (
            "xg_turned", "xgT_ready", "h1_ready", "h1T_ready", "y1_ready", "y1_kept", "y1_sent"))

        N_COND, N_CONST, N_V = 6, 3, 4

        block = ctx.enter_context(nc.Block())

        @block.sync
        def _(sp):
            def load(dst, src, s):
                sp.dma_start(dst, src).then_inc(s, 16)

            load(xT_sb[:], xT, in_cond)
            load(a_sb[:], lora_a, in_cond)
            load(wb_sb[:], w_base, in_cond)
            load(b_sb[:], lora_b, in_cond)
            load(bb_sb[:], b_base, in_cond)
            load(cr_sb[:], cond_rep, in_cond)
            load(cst[:], consts, in_const)
            load(rt_sb[:], router, in_const)
            load(crow[:].rearrange("o b e -> o (b e)"), cond_row, in_const)
            load(w1_sb[:], w1, in_w1)
            load(b1_sb[:], b1.to_broadcast((P, E * F)), in_w1)
            load(w2_sb[:], w2, in_w2)
            load(b2_sb[:], b2.to_broadcast((P, E * C)), in_w2)
            load(x_sb[:], x.rearrange("(c p) d -> p c d", p=P), in_x)
            load(dig_sb[:], digits.to_broadcast((P, STEPS * NJ)), in_x)
            load(pow_sb[:], powers.to_broadcast((P, STEPS)), in_x)
            for g in range(2):
                sp.wait_ge(c_tok_ready, g + 1)
                load(rows0.rearrange("(c p) d -> p c d", p=P)[:, 4 * g:4 * g + 4], c_tok[:, 4 * g:4 * g + 4],
                     rows0_written)
            sp.wait_ge(cexp_ready, 1)
            for b in range(NC):
                e = sp.value_load(cexp[0:1, b:b + 1], min_val=0, max_val=E - 1)
                load(cw_sb[:, b], cond_w[bass.ds(e, 1)].rearrange("o p w -> (o p) w"), in_cw)
            load(gw_sb[:], gate_w, in_gw)
            load(v1_sb[:].rearrange("p e f -> p (e f)"), v1, in_v)
            load(c1_sb[:], c1, in_v)
            load(v2_sb[:].rearrange("p e f c -> p (e f c)"), v2, in_v)
            load(c2b_sb[:].rearrange("p e c -> p (e c)"), c2b.to_broadcast((P, E * C)), in_v)
            sp.wait_ge(scattered, 16 * NB)
            for k in range(K):
                load(got[:, k], picked.rearrange("(k c p) d -> k p c d", p=P, k=K)[k], got_in)
            sp.wait_ge(x1_ready, NC)
            load(out.rearrange("(c p) d -> p c d", p=P), x1[:], out_init)
            sp.wait_ge(row_ready, NC)
            sp.wait_ge(sc_ready, 1)
            load(rows1.rearrange("(c p) d -> p c d", p=P), row[:], rows1_written)

        @block.gpsimd
        def _(pool):
            pool.wait_ge(idx_ready, 1)
            pool.wait_ge(rows0_written, 32)

            def scatter(b):
                pool.wait_ge(y_kept, b + 1)
                pool.indirect_dma_start(out=picked, out_offset=bass.IndirectOffsetOnAxis(ap=sidx[:, b:b + 1].bitcast(mybir.dt.uint32), axis=0),
                                        in_=y0[:, b], in_offset=None, bounds_check=K * T - 1,
                                        oob_is_err=False).then_inc(scattered, 16)

            LAG = 6
            for b in range(NB + LAG):
                if b < NB:
                    if b >= 2:
                        pool.wait_ge(x_turned, b - 1)
                    pool.indirect_dma_start(out=xs[:, b % 2], out_offset=None, in_=rows0,
                                            in_offset=bass.IndirectOffsetOnAxis(ap=gidx[:, b:b + 1].bitcast(mybir.dt.uint32), axis=0)
                                            ).then_inc(gathered[b % 2], 16)
                if b >= LAG:
                    scatter(b - LAG)

            pool.wait_ge(rows1_written, 16)
            for e in range(E):
                pool.wait_ge(idx1_ready, e + 1)
                for h in range(NH):
                    i = e * NH + h
                    pool.indirect_dma_start(out=xg[:, i], out_offset=None, in_=rows1,
                                            in_offset=bass.IndirectOffsetOnAxis(ap=idx1[:, i:i + 1].bitcast(mybir.dt.uint32), axis=0)
                                            ).then_inc(gathered1[e], 16)
            pool.wait_ge(out_init, 16)
            for e in range(E):
                pool.wait_ge(y1_kept, e + 1)
                if e:
                    pool.wait_ge(added[e - 1], 16 * NH)
                for h in range(NH):
                    i = e * NH + h
                    pool.indirect_dma_start(out=out, out_offset=bass.IndirectOffsetOnAxis(ap=idx1[:, i:i + 1].bitcast(mybir.dt.uint32), axis=0),
                                            in_=y1[:, e % 2, h], in_offset=None,
                                            compute_op=ALU.add).then_inc(added[e], 16)
            pool.wait_ge(added[E - 1], 16 * NH)

        @block.tensor
        def _(pe):
            ident = const("ident")

            pe.wait_ge(in_cond, 16 * N_COND)
            for g in range(2):
                pe.matmul(bank[g][:], a_sb[:], xT_sb[:, 512 * g:512 * g + 512], start=True, stop=True).then_inc(lora_h, 1)
            for g in range(2):
                pe.matmul(bank[2 + g][:], wb_sb[:], xT_sb[:, 512 * g:512 * g + 512], start=True, stop=False)
            for g in range(2):
                pe.wait_ge(lora_s, g + 1)
                pe.matmul(bank[2 + g][:], b_sb[:], hs[:, 512 * g:512 * g + 512], start=False, stop=True).then_inc(proj, 1)
            pe.wait_ge(in_const, 16 * N_CONST)
            for c in range(NC):
                if c % 4 == 0:
                    pe.wait_ge(cT_ready, c // 4 + 1)
                mm = pe.matmul(bank[4][:, E * c:E * c + E], cT[:, P * c:P * c + P], rt_sb[:], start=True, stop=True)
            mm.then_inc(logits, 1)
            for c in range(NC):
                mm = pe.transpose(bank[5 + c // 4][:, P * (c % 4):P * (c % 4) + P], cT[:, P * c:P * c + P], ident)
                if c % 4 == 3:
                    mm.then_inc(c_turned, 1)

            def running_counts(out_ap, m, width):
                pe.matmul(out_ap[:, 0:width], tri[:], m[:, 0:width], start=True, stop=True)
                for d in range(1, NC):
                    pe.matmul(out_ap[:, d * width:NC * width], ones[:], m[:, 0:(NC - d) * width],
                              start=(d == 1), stop=False)
                pe.matmul(out_ap[:, width:NC * width], tri[:], m[:, width:NC * width], start=False, stop=True)

            def totals(out_ap, m, width):
                for c in range(NC):
                    mm = pe.matmul(out_ap, ones[:], m[:, c * width:(c + 1) * width], start=(c == 0), stop=(c == NC - 1))
                return mm

            pe.wait_ge(mask_ready, 1)
            m0 = mask[:].rearrange("p c e -> p (c e)")
            running_counts(bank[7][:, 0:NC * E], m0, E)
            totals(bank[0][:, 0:E], m0, E).then_inc(prefix, 1)
            for i in range(K * NC):
                if i % NC == 0:
                    pe.wait_ge(onehots, i // NC + 1)
                mm = pe.matmul(bank[1][:, 0:2 * NBP], slot1h[:, i], blkv[:, i].rearrange("p v b -> p (v b)"),
                               start=(i == 0), stop=(i == K * NC - 1))
            mm.then_inc(slots, 1)

            pe.wait_ge(bexp_ready, 1)
            pe.wait_ge(in_w1, 32)
            pe.wait_ge(in_w2, 32)

            def turn_x(k, q):
                pe.wait_ge(gathered[q], 16 * (k // 2 + 1) if isinstance(k, int) else (k - q) * 8 + 16)
                pe.transpose(bank[q][:, 0:P], xs[:, q], ident).then_inc(x_turned, 1)

            def up(k, q, guard=True):
                e = pe.value_load(bexi[0:1, bass.ds(k, 1)], min_val=0, max_val=E - 1)
                pe.wait_ge(xsT_ready, k + 1)
                if guard:
                    pe.wait_ge(hb_ready, k - 1)
                pe.matmul(bank[2 + q][:], xsT[:, q], w1_sb[:, bass.ds(e * F, F)], start=True, stop=True).then_inc(h_ready, 1)

            def turn_h(k, q, guard=True):
                pe.wait_ge(hb_ready, k + 1)
                if guard:
                    pe.wait_ge(hT_ready, k - 1)
                for f in range(NF):
                    mm = pe.transpose(bank[4 + q][:, P * f:P * f + P], hb[:, q, P * f:P * f + P], ident)
                mm.then_inc(h_turned, 1)

            def down0(k, q, guard=True):
                e = pe.value_load(bexi[0:1, bass.ds(k, 1)], min_val=0, max_val=E - 1)
                pe.wait_ge(hT_ready, k + 1)
                if guard:
                    pe.wait_ge(y_kept, k - 1)
                for f in range(NF):
                    mm = pe.matmul(bank[6 + q][:, 0:C], hT[:, q, P * f:P * f + P],
                                   w2_sb[:, bass.ds(e * (NF * C) + f * C, C)], start=(f == 0), stop=(f == NF - 1))
                mm.then_inc(y_ready, 1)

            def step(k, q, n=None):
                n = k if n is None else n
                if n + 1 < NB:
                    turn_x(k + 1, 1 - q)
                if 0 <= n < NB:
                    up(k, q, n >= 2)
                if 0 <= n - 1 < NB:
                    turn_h(k - 1, 1 - q, n - 1 >= 2)
                if 0 <= n - 2 < NB:
                    down0(k - 2, q, n - 2 >= 2)

            for k in range(-1, 4):
                step(k, k % 2)
            with pe.Fori(2, (NB - 1) // 2) as i:
                step(2 * i, 0, 4)
                step(2 * i + 1, 1, 4)
            for k in range(NB - 1, NB + 2):
                step(k, k % 2)

            pe.wait_ge(in_cw, 16 * NC)

            def turn_x1(b):
                pe.wait_ge(x1_ready, b + 1)
                if b >= 2:
                    pe.wait_ge(x1T_ready, b - 1)
                pe.transpose(bank[b % 2][:, 0:P], x1[:, b], ident).then_inc(x1_turned, 1)

            def up_gate(b):
                pe.wait_ge(x1T_ready, b + 1)
                if b >= 2:
                    pe.wait_ge(hid_ready, b - 1)
                for m in range(4):
                    mm = pe.matmul(bank[2 + b % 2][:, P * m:P * m + P], cw_sb[:, b, P * m:P * m + P], x1T[:, b % 2],
                                   start=True, stop=True)
                mm.then_inc(upgate, 1)

            def down1(b):
                pe.wait_ge(hid_ready, b + 1)
                if b >= 2:
                    pe.wait_ge(dT_ready, b - 1)
                for h in range(2):
                    mm = pe.matmul(bank[4 + b % 2][:, 0:P], cw_sb[:, b, WD + P * h:WD + P * h + P],
                                   hid[:, b % 2, h], start=(h == 0), stop=(h == 1))
                mm.then_inc(down, 1)

            def turn_d(b):
                pe.wait_ge(dT_ready, b + 1)
                if b >= 1:
                    pe.wait_ge(row_ready, b)
                pe.transpose(bank[6][:, 0:P], dT[:, P * b:P * b + P], ident).then_inc(d_turned, 1)
                mm = pe.matmul(bank[7][:, E * b:E * b + E], dT[:, P * b:P * b + P], gw_sb[:], start=True, stop=True)
                return mm

            pe.wait_ge(in_gw, 16)
            for b in range(NC + 3):
                if b < NC:
                    turn_x1(b)
                if 0 <= b - 1 < NC:
                    up_gate(b - 1)
                if 0 <= b - 2 < NC:
                    down1(b - 2)
                if 0 <= b - 3 < NC:
                    mm = turn_d(b - 3)
            mm.then_inc(logits1, 1)

            with pe.Fori(0, STEPS) as s:
                pe.wait_ge(cmp_ready, s + 1)
                for c in range(NC):
                    mm = pe.matmul(bank[0][:, 0:E * NJ], ones[:], cmp_[:, c], start=(c == 0), stop=(c == NC - 1))
                mm.then_inc(counted, 1)

            pe.wait_ge(gteq_ready, 1)
            running_counts(bank[2][:, 0:NC * E], gteq[:, 0], E)
            running_counts(bank[3][:, 0:NC * E], gteq[:, 1], E)
            totals(bank[4][:, 0:E], gteq[:, 0], E).then_inc(prefix1, 1)

            def find_slots(e):
                pe.wait_ge(onehot1, e + 1)
                if e >= 2:
                    pe.wait_ge(idx1_ready, e - 1)
                for c in range(NC):
                    mm = pe.matmul(bank[(1, 5)[e % 2]][:, 0:2 * NH], one1[:, e % 2, c],
                                   hlfv[:, c, e].rearrange("p v h -> p (v h)"), start=(c == 0), stop=(c == NC - 1))
                mm.then_inc(slots1, 1)

            def turn_xg(e):
                pe.wait_ge(gathered1[e], 16 * NH)
                if e >= 1:
                    pe.wait_ge(xgT_ready, e)
                for h in range(NH):
                    mm = pe.transpose(bank[0][:, P * h:P * h + P], xg[:, e * NH + h, 0:C], ident)
                mm.then_inc(xg_turned, 1)

            def up1(e):
                pe.wait_ge(xgT_ready, e + 1)
                for f in range(NF):
                    g = 2 * (e % 2) + f // 2
                    if f % 2 == 0 and e >= 2:
                        pe.wait_ge(h1T_ready, 4 * (e - 2) + 2 * (f // 2) + 2)
                    mm = pe.matmul(bank[2 + g][:, CAP * (f % 2):CAP * (f % 2) + CAP], v1_sb[:, e, P * f:P * f + P],
                                   xgT[:, e % 2], start=True, stop=True)
                    if f % 2 == 1:
                        mm.then_inc(h1_ready, 1)

            def down_e(e):
                pe.wait_ge(h1T_ready, 4 * (e + 1))
                if e >= 2:
                    pe.wait_ge(y1_ready, e - 1)
                for h in range(NH):
                    for f in range(NF):
                        mm = pe.matmul(bank[6 + e % 2][:, C * h:C * h + C], h1T[:, e % 2, f, P * h:P * h + P],
                                       v2_sb[:, e, f], start=(f == 0), stop=(f == NF - 1))
                mm.then_inc(y1_sent, 1)

            pe.wait_ge(in_v, 16 * N_V)
            for e in range(E):
                find_slots(e)
            turn_xg(0)
            for e in range(E + 1):
                if e == 1:
                    pe.wait_ge(idx1_ready, E)
                if e < E:
                    up1(e)
                if e + 1 < E:
                    turn_xg(e + 1)
                if e >= 1:
                    down_e(e - 1)

        @block.scalar
        def _(act):
            for g in range(2):
                act.wait_ge(proj, g + 1)
                act.activation(cT[:, 512 * g:512 * g + 512], bank[2 + g][:], ACT.Identity, bias=bb_sb[:]).then_inc(cT_ready, 1)
            for g in range(2):
                act.wait_ge(c_turned, g + 1)
                act.activation(c_tok[:, 4 * g:4 * g + 4].rearrange("p c d -> p (c d)"), bank[5 + g][:], ACT.Copy).then_inc(c_tok_ready, 1)
            act.wait_ge(shift_ready, 1)
            act.activation(expd[:], shifted[:], ACT.Exp).then_inc(exp_ready, 1)
            act.activation(den[:], dif2[:], ACT.Exp).then_inc(exp_ready, 1)

            def take_x(k, q, guard=True):
                act.wait_ge(x_turned, k + 1)
                if guard:
                    act.wait_ge(h_ready, k - 1)
                act.activation(xsT[:, q], bank[q][:, 0:P], ACT.Copy).then_inc(xsT_ready, 1)

            def take_h(k, q, guard=True):
                act.wait_ge(h_turned, k + 1)
                if guard:
                    act.wait_ge(y_ready, k - 1)
                act.activation(hT[:, q], bank[4 + q][:], ACT.Relu).then_inc(hT_ready, 1)

            def step(k, q, n=None):
                n = k if n is None else n
                if n + 1 < NB:
                    take_x(k + 1, 1 - q, n + 1 >= 2)
                if 0 <= n - 1 < NB:
                    take_h(k - 1, 1 - q, n - 1 >= 2)

            for k in range(-1, 4):
                step(k, k % 2)
            with act.Fori(2, (NB - 1) // 2) as i:
                step(2 * i, 0, 4)
                step(2 * i + 1, 1, 4)
            for k in range(NB - 1, NB + 1):
                step(k, k % 2)

            def take_x1(b):
                act.wait_ge(x1_turned, b + 1)
                if b >= 2:
                    act.wait_ge(upgate, b - 1)
                act.activation(x1T[:, b % 2], bank[b % 2][:, 0:P], ACT.Copy).then_inc(x1T_ready, 1)

            def silu(b):
                act.wait_ge(upgate, b + 1)
                if b >= 2:
                    act.wait_ge(hid_ready, b - 1)
                for h in range(2):
                    ins = act.activation(su[:, b % 2, h], bank[2 + b % 2][:, P * h:P * h + P], ACT.Silu,
                                         bias=cw_sb[:, b, BU + h:BU + h + 1])
                ins.then_inc(silu_ready, 1)

            def take_d(b):
                act.wait_ge(down, b + 1)
                act.activation(dT[:, P * b:P * b + P], bank[4 + b % 2][:, 0:P], ACT.Identity,
                               bias=cw_sb[:, b, BD:BD + 1]).then_inc(dT_ready, 1)

            def take_row(b):
                act.wait_ge(d_turned, b + 1)
                act.activation(row[:, b, 0:C], bank[6][:, 0:P], ACT.Copy).then_inc(row_ready, 1)

            for b in range(NC + 3):
                if b < NC:
                    take_x1(b)
                if 0 <= b - 1 < NC:
                    silu(b - 1)
                if 0 <= b - 2 < NC:
                    take_d(b - 2)
                if 0 <= b - 3 < NC:
                    take_row(b - 3)
            act.wait_ge(logits1, 1)
            act.activation(th[:].rearrange("p c e -> p (c e)"), bank[7][:, 0:NC * E], ACT.Tanh, scale=0.5).then_inc(tanh_ready, 1)

            def take_xg(e):
                act.wait_ge(xg_turned, e + 1)
                if e >= 2:
                    act.wait_ge(h1_ready, 2 * (e - 1))
                act.activation(xgT[:, e % 2], bank[0][:, 0:CAP], ACT.Copy).then_inc(xgT_ready, 1)

            def gelu(e):
                if e >= 2:
                    act.wait_ge(y1_sent, e - 1)
                for f in range(NF):
                    if f % 2 == 0:
                        act.wait_ge(h1_ready, 2 * e + f // 2 + 1)
                    act.activation(h1T[:, e % 2, f], bank[2 + 2 * (e % 2) + f // 2][:, CAP * (f % 2):CAP * (f % 2) + CAP],
                                   ACT.Gelu, bias=c1_sb[:, e * NF + f:e * NF + f + 1]).then_inc(h1T_ready, 1)

            take_xg(0)
            for e in range(E):
                gelu(e)
                if e + 1 < E:
                    take_xg(e + 1)

        @block.vector
        def _(v):
            done = [0]

            def link(ins):
                done[0] = done[0] + 1
                ins.then_inc(dve, 1)
                v.wait_ge(dve, done[0])

            def bc(ap, dim, n):
                return ap.unsqueeze(dim).to_broadcast([*ap.shape[:dim], n, *ap.shape[dim:]])

            def int_sum(out_ap, in_ap):
                with nc.allow_low_precision(reason="integers, exact in float32"):
                    return v.tensor_reduce(out_ap, in_ap, AX.X, ALU.add)

            link(v.memset(ones[:], 1.0))
            v.wait_ge(in_cond, 16 * N_COND)
            link(v.tensor_scalar(cr2[:], cr_sb[:], LORA_SCALE, None, ALU.mult))
            for g in range(2):
                v.wait_ge(lora_h, g + 1)
                v.tensor_tensor(hs[:, 512 * g:512 * g + 512].rearrange("p (c t) -> p c t", t=P),
                                bank[g][:].rearrange("p (c t) -> p c t", t=P),
                                bc(cr2[:, 4 * g:4 * g + 4], 2, P), ALU.mult).then_inc(lora_s, 1)
            v.wait_ge(in_const, 16 * N_CONST)
            v.tensor_copy(tri[:], const("tri"))
            link(v.tensor_copy(iota[:], const("iota")))

            link(v.tensor_reduce(cmax[:], crow[:], AX.X, ALU.max))
            link(v.tensor_tensor(carg[:], crow[:], bc(cmax[:], 2, E), ALU.is_equal))
            link(v.tensor_tensor(carg[:], carg[:], bc(const("rev")[0:1], 1, NC), ALU.mult))
            link(v.tensor_reduce(cmax[:], carg[:], AX.X, ALU.max))
            v.tensor_scalar(cexp[:], cmax[:], -1.0, float(E), ALU.mult, ALU.add).then_inc(cexp_ready, 1)

            v.wait_ge(logits, 1)
            link(v.tensor_copy(lg[:].rearrange("p c e -> p (c e)"), bank[4][:, 0:NC * E]))
            for k in range(K):
                src = (lg, lg2)[k]
                link(v.tensor_reduce(top[:, k], src[:], AX.X, ALU.max))
                link(v.tensor_tensor(eq[:], src[:], bc(top[:, k], 2, E), ALU.is_equal))
                link(v.tensor_tensor(eq[:], eq[:], bc(const("rev"), 1, NC), ALU.mult))
                link(v.tensor_reduce(mr[:], eq[:], AX.X, ALU.max))
                link(v.tensor_tensor(sel[:, k], eq[:], bc(mr[:], 2, E), ALU.is_equal))
                if k == 0:
                    link(v.scalar_tensor_tensor(lg2[:], sel[:, 0], NEG, lg[:], ALU.mult, ALU.add))
            v.tensor_tensor(mask[:], sel[:, 0], sel[:, 1], ALU.add).then_inc(mask_ready, 1)
            v.tensor_tensor(dif2[:], top[:, 1], top[:, 0], ALU.subtract)
            v.tensor_tensor(shifted[:], lg[:], bc(top[:, 0], 2, E), ALU.subtract).then_inc(shift_ready, 1)

            v.wait_ge(prefix, 1)
            link(v.tensor_tensor(nbig[:], bc(bank[0][:, 0:E], 2, E), bc(const("blk0"), 1, E), ALU.is_gt))
            link(v.tensor_reduce(nblk[:], nbig[:], AX.X, ALU.add))
            link(v.tensor_tensor(before[:], bc(nblk[:], 1, E), const("lt").rearrange("p (a b) -> p a b", b=E), ALU.mult))
            link(v.tensor_reduce(cblk[:], before[:], AX.X, ALU.add))
            v.tensor_scalar(base[:], cblk[:], float(P), None, ALU.mult)
            link(v.tensor_tensor(cinc[:], cblk[:], nblk[:], ALU.add))
            link(v.tensor_tensor(pos[:], bank[7][:, 0:NC * E].rearrange("p (c e) -> p c e", e=E), bc(base[:], 1, NC), ALU.add))
            for k in range(K):
                ins = v.tensor_tensor(psel[:, k], sel[:, k], pos[:], ALU.mult)
            link(ins)
            link(int_sum(posk[:], psel[:].rearrange("p k c e -> p (k c) e")))
            v.tensor_scalar(blk[:], posk[:], 7, None, ALU.logical_shift_right)
            link(v.tensor_scalar(loc[:], posk[:], P - 1, None, ALU.bitwise_and))
            link(v.tensor_tensor(blk1h[:], bc(iota[:, 0:NBP], 1, K * NC), bc(blk[:], 2, NBP), ALU.is_equal))
            v.tensor_scalar(blkv[:, :, 0], blk1h[:], const("pcol"), None, ALU.mult)
            v.tensor_tensor(blkv[:, :, 1], blk1h[:], bc(const("dval"), 2, NBP), ALU.mult)
            for i in range(K * NC):
                ins = v.tensor_scalar(slot1h[:, i], iota[:], loc[:, i:i + 1], None, ALU.is_equal)
                if i % NC == NC - 1:
                    ins.then_inc(onehots, 1)
            link(v.tensor_tensor(bexp[:], bc(cinc[0:1], 1, NBP), bc(iota[0:1, 0:NBP], 2, E), ALU.is_le))
            link(v.tensor_reduce(bexf[:], bexp[:], AX.X, ALU.add))
            v.tensor_scalar(bexi[:], bexf[:], float(E - 1), None, ALU.min).then_inc(bexp_ready, 1)
            v.wait_ge(slots, 1)
            link(v.tensor_reduce(idxf[:], bank[1][:, 0:2 * NBP].rearrange("p (v b) -> p b v", v=2), AX.X, ALU.add))
            link(v.tensor_scalar(sidx[:], idxf[:], float(PAD), None, ALU.add))
            v.tensor_scalar(gidx[:], sidx[:], T - 1, None, ALU.bitwise_and).then_inc(idx_ready, 1)

            v.wait_ge(in_w1, 32)
            v.wait_ge(in_w2, 32)

            def add_b1(k, q, guard=True):
                e = v.value_load(bexi[0:1, bass.ds(k, 1)], min_val=0, max_val=E - 1)
                v.wait_ge(h_ready, k + 1)
                if guard:
                    v.wait_ge(h_turned, k - 1)
                v.tensor_tensor(hb[:, q], bank[2 + q][:], b1_sb[:, bass.ds(e * F, F)], ALU.add).then_inc(hb_ready, 1)

            def add_b2(k, q):
                e = v.value_load(bexi[0:1, bass.ds(k, 1)], min_val=0, max_val=E - 1)
                v.wait_ge(y_ready, k + 1)
                v.tensor_tensor(y0[:, bass.ds(k, 1)].rearrange("p o c -> p (o c)"), bank[6 + q][:, 0:C],
                                b2_sb[:, bass.ds(e * C, C)], ALU.add).then_inc(y_kept, 1)

            def step(k, q, n=None):
                n = k if n is None else n
                if 0 <= n < NB:
                    add_b1(k, q, n >= 2)
                if 0 <= n - 2 < NB:
                    add_b2(k - 2, q)

            v.wait_ge(bexp_ready, 1)
            for k in range(0, 4):
                step(k, k % 2)
            with v.Fori(2, (NB - 1) // 2) as i:
                step(2 * i, 0, 4)
                step(2 * i + 1, 1, 4)
            for k in range(NB - 1, NB + 2):
                step(k, k % 2)

            v.wait_ge(exp_ready, 2)
            link(v.tensor_reduce(zsum[:], expd[:], AX.X, ALU.add))
            link(v.scalar_tensor_tensor(den2[:], zsum[:], 1e-9, den[:], ALU.mult, ALU.add))
            link(v.tensor_scalar(den2[:], den2[:], 1.0, None, ALU.add))
            link(v.reciprocal(wt[:, 0], den2[:]))
            link(v.tensor_tensor(wt[:, 1], wt[:, 0], den[:], ALU.mult))
            v.wait_ge(in_x, 48)
            v.wait_ge(got_in, 32)
            for c in range(NC):
                link(v.scalar_tensor_tensor(xa[:, c], got[:, 0, c], wt[:, 0, c:c + 1], x_sb[:, c], ALU.mult, ALU.add))
                v.scalar_tensor_tensor(x1[:, c], got[:, 1, c], wt[:, 1, c:c + 1], xa[:, c], ALU.mult, ALU.add).then_inc(x1_ready, 1)

            v.wait_ge(in_cw, 16 * NC)
            for b in range(NC):
                v.wait_ge(silu_ready, b + 1)
                if b >= 2:
                    v.wait_ge(down, b - 1)
                for h in range(2):
                    ins = v.scalar_tensor_tensor(hid[:, b % 2, h], bank[2 + b % 2][:, P * (2 + h):P * (3 + h)],
                                                 cw_sb[:, b, BG + h:BG + h + 1], su[:, b % 2, h], ALU.add, ALU.mult)
                ins.then_inc(hid_ready, 1)

            v.wait_ge(tanh_ready, 1)
            link(v.tensor_scalar(sc[:], th[:], 1.0, 0.5, ALU.add, ALU.mult))
            v.tensor_copy(row[:, :, C:ROW], sc[:]).then_inc(sc_ready, 1)

            link(v.memset(tau[:], 0))
            first = done[0]
            PER = 4
            with v.Fori(0, STEPS) as s:
                done[0] = first + s * PER
                link(v.tensor_tensor(thr[:], bc(tau[:], 2, NJ), bc(dig_sb[:, bass.ds(s * NJ, NJ)], 1, E), ALU.bitwise_or))
                v.tensor_tensor(cmp_[:].rearrange("p c (e j) -> p c e j", j=NJ), bc(sc[:], 3, NJ),
                                bc(thr[:].bitcast(F32), 1, NC), ALU.is_ge).then_inc(cmp_ready, 1)
                v.wait_ge(counted, s + 1)
                link(v.tensor_scalar(flag[:].rearrange("p e j -> p (e j)"), bank[0][:, 0:E * NJ], float(CAP),
                                     pow_sb[:, bass.ds(s, 1)], ALU.is_ge, ALU.mult))
                link(int_sum(inc[:], flag[:]))
                link(v.tensor_tensor(tau[:], tau[:], inc[:], ALU.bitwise_or))
            done[0] = first + STEPS * PER

            tauf = tau[:].bitcast(F32)
            gt = gteq[:, 0].rearrange("p (c e) -> p c e", e=E)
            at = gteq[:, 1].rearrange("p (c e) -> p c e", e=E)
            v.tensor_tensor(gt, sc[:], bc(tauf, 1, NC), ALU.is_gt)
            ins = v.tensor_tensor(at, sc[:], bc(tauf, 1, NC), ALU.is_equal)
            ins.then_inc(gteq_ready, 1)
            v.wait_ge(prefix1, 1)
            v.tensor_copy(ngt[:], bank[4][:, 0:E])
            link(v.tensor_tensor(pg_[:], bank[2][:, 0:NC * E].rearrange("p (c e) -> p c e", e=E), gt, ALU.mult))
            link(v.tensor_tensor(pe_[:], bank[3][:, 0:NC * E].rearrange("p (c e) -> p c e", e=E), bc(ngt[:], 1, NC), ALU.add))
            link(v.tensor_tensor(pe_[:], pe_[:], at, ALU.mult))
            link(v.tensor_tensor(pos1[:], pg_[:], pe_[:], ALU.add))
            link(v.tensor_tensor(pg_[:], gt, at, ALU.add))
            link(v.tensor_scalar(pg_[:], pg_[:], -float(T), float(T), ALU.mult, ALU.add))
            link(v.tensor_tensor(posi[:].rearrange("p (c e) -> p c e", e=E), pos1[:], pg_[:], ALU.add))
            v.tensor_scalar(half[:], posi[:], 7, None, ALU.logical_shift_right)
            link(v.tensor_scalar(loc1[:], posi[:], P - 1, None, ALU.bitwise_and))
            link(v.tensor_tensor(hlf1h[:], bc(iota[:, 0:NH], 1, NC * E), bc(half[:], 2, NH), ALU.is_equal))
            v.tensor_scalar(hlfv[:, :, :, 0].rearrange("p c e h -> p (c e) h"), hlf1h[:], const("pcol"), None, ALU.mult)
            v.tensor_tensor(hlfv[:, :, :, 1].rearrange("p c e h -> p c e h"), hlf1h[:].rearrange("p (c e) h -> p c e h", e=E),
                            bc(bc(const("cval"), 2, E), 3, NH), ALU.mult)
            def place(e):
                if e >= 2:
                    v.wait_ge(slots1, e - 1)
                for c in range(NC):
                    ins = v.tensor_scalar(one1[:, e % 2, c], iota[:], loc1[:, c * E + e:c * E + e + 1], None, ALU.is_equal)
                ins.then_inc(onehot1, 1)

            def index(e):
                v.wait_ge(slots1, e + 1)
                int_sum(idx1[:, NH * e:NH * e + NH],
                        bank[(1, 5)[e % 2]][:, 0:2 * NH].rearrange("p (v h) -> p h v", v=2)).then_inc(idx1_ready, 1)

            for e in range(E + 1):
                if e < E:
                    place(e)
                if e:
                    index(e - 1)

            v.wait_ge(in_v, 16 * N_V)
            for e in range(E):
                v.wait_ge(y1_sent, e + 1)
                if e >= 2:
                    v.wait_ge(added[e - 2], 16 * NH)
                ins = v.tensor_tensor(yb[:, e % 2], bank[6 + e % 2][:, 0:NH * C].rearrange("p (h c) -> p h c", c=C),
                                      bc(c2b_sb[:, e], 1, NH), ALU.add)
                ins.then_inc(y1_ready, 1)
                v.wait_ge(y1_ready, e + 1)
                for h in range(NH):
                    ins = v.tensor_scalar(y1[:, e % 2, h], yb[:, e % 2, h], xg[:, e * NH + h, C + e:C + e + 1], None, ALU.mult)
                ins.then_inc(y1_kept, 1)


def kernel(x, cond_8, L0_cond_W_base, L0_cond_b_base, L0_cond_As, L0_cond_Bs, L0_ffn_router_w, L0_ffn_w1,
           L0_ffn_b1, L0_ffn_w2, L0_ffn_b2, L1_cond_W_up, L1_cond_b_up, L1_cond_W_gate, L1_cond_b_gate,
           L1_cond_W_down, L1_cond_b_down, L1_ffn_Wg, L1_ffn_W1, L1_ffn_b1, L1_ffn_W2, L1_ffn_b2):
    import concourse.bacc as _bacc
    from concourse.bass_utils import run_bass_kernel_spmd as _run

    a = np.asarray
    table, digits, powers = constants()
    xf = a(x).reshape(T, C)
    parts = (P, E, F // P, C)
    cond_w = np.concatenate([
        a(L1_cond_W_up).transpose(0, 2, 1), a(L1_cond_W_gate).transpose(0, 2, 1),
        a(L1_cond_W_down).transpose(0, 2, 1).reshape(E, 2, P, C).transpose(0, 2, 1, 3).reshape(E, P, 2 * C),
        a(L1_cond_b_up).reshape(E, 2, P).transpose(0, 2, 1), a(L1_cond_b_gate).reshape(E, 2, P).transpose(0, 2, 1),
        a(L1_cond_b_down).reshape(E, P, 1)], axis=2)
    laid_out = {
        "xT": xf.T,
        "x": xf,
        "lora_a": a(L0_cond_As).reshape(E * R, C).T,
        "lora_b": a(L0_cond_Bs).transpose(0, 2, 1).reshape(E * R, C),
        "w_base": a(L0_cond_W_base).T,
        "b_base": a(L0_cond_b_base).reshape(C, 1),
        "cond_rep": np.repeat(a(cond_8).T, R, axis=0),
        "cond_row": a(cond_8).reshape(1, NC * E),
        "router": a(L0_ffn_router_w).T,
        "w1": a(L0_ffn_w1).transpose(2, 0, 1).reshape(C, E * F),
        "b1": a(L0_ffn_b1).reshape(1, E * F),
        "w2": a(L0_ffn_w2).transpose(2, 0, 1).reshape(NF, P, E, C).transpose(1, 2, 0, 3).reshape(P, E * NF * C),
        "b2": a(L0_ffn_b2).reshape(1, E * C),
        "cond_w": cond_w,
        "gate_w": a(L1_ffn_Wg),
        "v1": a(L1_ffn_W1).transpose(1, 0, 2).reshape(C, E * F),
        "c1": a(L1_ffn_b1).reshape(E, NF, P).transpose(2, 0, 1).reshape(P, E * NF),
        "v2": a(L1_ffn_W2).reshape(E, NF, P, C).transpose(2, 0, 1, 3).reshape(P, E * NF * C),
        "c2b": a(L1_ffn_b2).reshape(1, E * C),
        "consts": table,
        "digits": digits,
        "powers": powers,
    }
    nc = _bacc.Bacc("TRN2", target_bir_lowering=False, num_devices=1)
    arrays, args = {}, []
    for name, v in laid_out.items():
        v = np.ascontiguousarray(v)
        arrays[f"in_{name}"] = v
        args.append(nc.dram_tensor(f"in_{name}", v.shape, mybir.dt.from_np(v.dtype), kind="ExternalInput").ap())
    args.append(nc.dram_tensor("out_x", (T, C), F32, kind="ExternalOutput").ap())
    adaln_moe(nc, *args)
    r = _run(nc, [arrays], core_ids=[0])
    return r.results[0]["out_x"].reshape(NC, P, C)
```

```python
from contextlib import ExitStack

import numpy as np

import concourse.bass as bass
from concourse import mybir

P = 128
T, C = 1024, 128
NC = T // P
E = 8
R = 16
F = 512
NF = F // P
H = 256
K = 2
LORA_SCALE = 32.0 / R
RING = 4
NB = K * T // P + E - 1
MIN_GROUPS = K * T // P // RING
MAX_GROUPS = -(-NB // RING)
NBP = MAX_GROUPS * RING
CAP = 256
NH = CAP // P
PAD = 4096
ROW = C + E
NJ = 8
STEPS = 9
NEG = -3.0e38

F32 = mybir.dt.float32
BF16 = mybir.dt.bfloat16
I32 = mybir.dt.int32
U32 = mybir.dt.uint32
ALU = mybir.AluOpType
ACT = mybir.ActivationFunctionType
AX = mybir.AxisListType

_WIDTHS = [("ident", P), ("tri", P), ("iota", P), ("rev", E), ("pcol", 1), ("blk0", E), ("lt", E * E),
           ("dval", K * NC), ("cval", NC), ("digits", STEPS * NJ)]
_AT, _n = {}, 0
for _name, _w in _WIDTHS:
    _AT[_name] = (_n, _n + _w)
    _n += _w
CONSTS = _n
WU, WG, WD, BU, BG, BD = 0, H, 2 * H, 3 * H, 3 * H + 2, 3 * H + 4
CW = 3 * H + 5


def constants():
    t = np.zeros((P, CONSTS), np.float32)
    p = np.arange(P)

    def put(name, v):
        a, b = _AT[name]
        t[:, a:b] = v

    put("ident", np.eye(P))
    put("tri", p[:, None] < p[None, :])
    put("iota", p[None, :])
    put("rev", E - np.arange(E)[None, :])
    put("pcol", p[:, None])
    put("blk0", P * np.arange(E)[None, :])
    e = np.arange(E)
    put("lt", (e[None, :] < e[:, None]).reshape(1, -1))
    k, c = np.meshgrid(np.arange(K), np.arange(NC), indexing="ij")
    put("dval", (P * c + T * k - PAD).reshape(1, -1))
    put("cval", P * np.arange(NC)[None, :])
    put("digits", (np.arange(NJ)[None, :] * 0.5 / NJ ** np.arange(STEPS)[:, None]).reshape(1, -1))
    return t


def adaln_moe(nc, xT, x, lora_a, lora_b, w_base, b_base, cond_rep, cond_row, router, w1, b1, w2, b2,
              cond_w, gate_w, v1, c1, v2, c2b, consts, out):
    with ExitStack() as ctx:
        def sb(name, shape, dt=F32):
            return ctx.enter_context(nc.sbuf_tensor(name, shape, dt))

        def sem(name):
            return ctx.enter_context(nc.semaphore(name))

        rows0 = nc.dram_tensor("rows0", (T, C), F32).ap()
        rows1 = nc.dram_tensor("rows1", (T, ROW), F32).ap()
        picked = nc.dram_tensor("picked", (K * T, C), F32).ap()

        bank = [ctx.enter_context(nc.psum_tensor(f"bank{i}", [P, 512], F32)) for i in range(8)]

        xT_sb = sb("xT_sb", [P, T])
        x_sb = sb("x_sb", [P, NC, C])
        a_sb = sb("a_sb", [P, E * R])
        b_sb = sb("b_sb", [P, C])
        wb_sb = sb("wb_sb", [P, C])
        bb_sb = sb("bb_sb", [P, 1])
        cr_sb = sb("cr_sb", [P, NC])
        crow = sb("crow", [1, NC, E])
        rt_sb = sb("rt_sb", [P, E])
        w1_sb = sb("w1_sb", [P, E * F])
        b1_sb = sb("b1_sb", [P, E * F])
        w2_sb = sb("w2_sb", [P, E * NF * C])
        b2_sb = sb("b2_sb", [P, E * C])
        cw_sb = sb("cw_sb", [P, NC, CW])
        gw_sb = sb("gw_sb", [P, E])
        v1_sb = sb("v1_sb", [P, E, F])
        c1_sb = sb("c1_sb", [P, E * NF])
        v2_sb = sb("v2_sb", [P, E, NF, C])
        c2b_sb = sb("c2b_sb", [P, E, C])
        cst = sb("cst", [P, CONSTS])
        b1_row = v1_sb[0:1].rearrange("p e f -> p (e f)")
        b2_row = v2_sb[0:1, 0:2].rearrange("p e f c -> p (e f c)")
        c2b_row = v2_sb[0:1, 2:4].rearrange("p e f c -> p (e f c)")

        def const(name):
            a, b = _AT[name]
            return cst[:, a:b]

        tri = sb("tri", [P, P], BF16)
        iota = sb("iota", [P, P], BF16)
        ones = sb("ones", [P, P], BF16)

        cr2 = sb("cr2", [P, NC])
        hs = sb("hs", [P, T])
        cT = sb("cT", [P, T])
        c_tok = sb("c_tok", [P, NC, C])
        lg = sb("lg", [P, NC, E])
        lg2 = sb("lg2", [P, NC, E])
        eq = sb("eq", [P, NC, E])
        top = sb("top", [P, K, NC])
        mr = sb("mr", [P, NC])
        sel = sb("sel", [P, K, NC, E])
        mask = sb("mask", [P, NC, E], BF16)
        nbig = sb("nbig", [P, E, E])
        nblk = sb("nblk", [P, E])
        before = sb("before", [P, E, E])
        cblk = sb("cblk", [P, E])
        cinc = sb("cinc", [P, E])
        base = sb("base", [P, E])
        pos = sb("pos", [P, NC, E])
        psel = sb("psel", [P, K, NC, E])
        posk = sb("posk", [P, K * NC], I32)
        blk = sb("blk", [P, K * NC], I32)
        loc = sb("loc", [P, K * NC], I32)
        slot1h = sb("slot1h", [P, K * NC, P], BF16)
        blk1h = sb("blk1h", [P, K * NC, NBP], BF16)
        blkv = sb("blkv", [P, K * NC, 2, NBP], BF16)
        idxf = sb("idxf", [P, NBP])
        sidx = sb("sidx", [P, NBP], I32)
        gidx = sb("gidx", [P, NBP], I32)
        bexp = sb("bexp", [1, NBP, E])
        bexf = sb("bexf", [1, NBP])
        bexi = sb("bexi", [1, NBP], I32)
        nall = sb("nall", [1, 1], I32)
        more = sb("more", [1, 1], I32)
        shifted = sb("shifted", [P, NC, E])
        expd = sb("expd", [P, NC, E])
        zsum = sb("zsum", [P, NC])
        dif2 = sb("dif2", [P, NC])
        scrap = sb("scrap", [P, 1])
        wt = sb("wt", [P, K, NC])
        den = sb("den", [P, NC])
        den2 = sb("den2", [P, NC])

        xs = sb("xs", [P, RING, C])
        xsT = sb("xsT", [P, 2, P])
        hb = sb("hb", [P, 2, F])
        hT = sb("hT", [P, 2, F])
        y0 = sb("y0", [P, NBP, C])
        got = b1_sb[:, 0:K * NC * C].rearrange("p (k c d) -> p k c d", k=K, c=NC)
        xa = hs[:].rearrange("p (c d) -> p c d", c=NC)
        x1 = c_tok

        carg = sb("carg", [1, NC, E])
        cmax = sb("cmax", [1, NC])
        cexp = sb("cexp", [1, NC], I32)
        x1T = sb("x1T", [P, 2, P])
        su = sb("su", [P, 2, 2, P])
        hid = sb("hid", [P, 2, 2, P])
        dT = cT
        row = sb("row", [P, NC, ROW])
        th = sb("th", [P, NC, E])
        sc = sb("sc", [P, NC, E])
        tau = sb("tau", [P, E])
        thr = sb("thr", [P, NJ, E])
        cmp_ = sb("cmp", [P, NC, NJ * E], BF16)
        reach = sb("reach", [P, NJ, E])
        gteq = sb("gteq", [P, 2, NC * E], BF16)
        ngt = sb("ngt", [P, E])
        pe_ = sb("pe_", [P, NC, E])
        pg_ = sb("pg_", [P, NC, E])
        pos1 = sb("pos1", [P, NC, E])
        posi = sb("posi", [P, NC * E], I32)
        half = sb("half", [P, NC * E], I32)
        loc1 = sb("loc1", [P, NC * E], I32)
        one1 = slot1h[:].rearrange("p (r c) s -> p r c s", r=2)
        hlf1h = sb("hlf1h", [P, NC * E, NH], BF16)
        hlfv = sb("hlfv", [P, NC, E, 2, NH], BF16)
        idx1 = sb("idx1", [P, E * NH], I32)
        xg = sb("xg", [P, E * NH, ROW])
        xgT = sb("xgT", [P, 2, CAP])
        h1T = b1_sb[:, K * NC * C:].rearrange("p (r f s) -> p r f s", r=2, f=NF)
        yb = sb("yb", [P, 2, NH, C])
        y1 = sb("y1", [P, 2, NH, C])

        in_cond, in_const, in_w1, in_w2, in_x, in_cw = (sem(n) for n in (
            "in_cond", "in_const", "in_w1", "in_w2", "in_x", "in_cw"))
        in_gw, in_v, in_rows, spread = sem("in_gw"), sem("in_v"), sem("in_rows"), sem("spread")
        dve = sem("dve_steps")
        consts_ready = sem("consts_ready")
        cexp_ready = sem("cexp_ready")
        lora_h, lora_s, proj, cT_ready, logits = (sem(n) for n in (
            "lora_h", "lora_s", "proj", "cT_ready", "logits"))
        c_turned, c_tok_ready, rows0_written = sem("c_turned"), sem("c_tok_ready"), sem("rows0_written")
        mask_ready, prefix, onehots, slots = (sem(n) for n in ("mask_ready", "prefix", "onehots", "slots"))
        idx_ready, bexp_ready, shift_ready, exp_ready = (sem(n) for n in (
            "idx_ready", "bexp_ready", "shift_ready", "exp_ready"))
        gathered = [sem(f"gathered_{q}") for q in range(RING)]
        x_turned, xsT_ready, h_ready, hb_ready, h_turned, hT_ready, y_ready, y_kept, scattered, xa_ready = (
            sem(n) for n in ("x_turned", "xsT_ready", "h_ready", "hb_ready", "h_turned", "hT_ready",
                             "y_ready", "y_kept", "scattered", "xa_ready"))
        got_in = [sem(f"got_in_{h}") for h in range(2)]
        x1_ready, x1_turned, x1T_ready, upgate, silu_ready, hid_ready, down, dT_ready = (sem(n) for n in (
            "x1_ready", "x1_turned", "x1T_ready", "upgate", "silu_ready", "hid_ready", "down", "dT_ready"))
        d_turned, row_ready, logits1, tanh_ready, sc_ready, rows1_written, out_init = (sem(n) for n in (
            "d_turned", "row_ready", "logits1", "tanh_ready", "sc_ready", "rows1_written", "out_init"))
        cmp_ready, counted, gteq_ready, prefix1, onehot1, slots1, idx1_ready = (sem(n) for n in (
            "cmp_ready", "counted", "gteq_ready", "prefix1", "onehot1", "slots1", "idx1_ready"))
        gathered1 = [sem(f"gathered1_{e}") for e in range(E)]
        added = [sem(f"added_{e}") for e in range(E)]
        xg_turned, xgT_ready, h1_ready, h1T_ready, y1_ready, y1_kept, y1_sent = (sem(n) for n in (
            "xg_turned", "xgT_ready", "h1_ready", "h1T_ready", "y1_ready", "y1_kept", "y1_sent"))

        N_COND, N_CONST = 6, 3
        AHEAD = 3

        def run_blocks(eng, groups, stages):
            def step(k, q, first, last=0):
                for i, work in stages:
                    if first >= i >= last:
                        work(k - i, (q - i) % RING, first - i)

            for k in range(RING):
                step(k, k, k)
            with eng.Fori(1, groups) as g:
                for q in range(RING):
                    step(RING * g + q, q, NBP)
            for j in range(max(i for i, _ in stages)):
                step(groups * RING + j, j, NBP, last=j + 1)

        block = ctx.enter_context(nc.Block())

        @block.sync
        def _(sp):
            def load(dst, src, s):
                sp.dma_start(dst, src).then_inc(s, 16)

            load(xT_sb[:], xT, in_cond)
            load(a_sb[:], lora_a, in_cond)
            load(wb_sb[:], w_base, in_cond)
            load(b_sb[:], lora_b, in_cond)
            load(bb_sb[:], b_base, in_cond)
            load(cr_sb[:], cond_rep, in_cond)
            load(cst[:], consts, in_const)
            load(rt_sb[:], router, in_const)
            load(crow[:].rearrange("o b e -> o (b e)"), cond_row, in_const)
            load(b1_row, b1, in_rows)
            load(b2_row, b2, in_rows)
            load(c2b_row, c2b, in_rows)
            load(w1_sb[:], w1, in_w1)
            load(w2_sb[:], w2, in_w2)

            def load_cond(b):
                e = sp.value_load(cexp[0:1, b:b + 1], min_val=0, max_val=E - 1)
                load(cw_sb[:, b], cond_w[bass.ds(e, 1)].rearrange("o p w -> (o p) w"), in_cw)

            sp.wait_ge(cexp_ready, 1)
            load_cond(0)
            for g in range(2):
                sp.wait_ge(c_tok_ready, g + 1)
                load(rows0.rearrange("(c p) d -> p c d", p=P)[:, 4 * g:4 * g + 4], c_tok[:, 4 * g:4 * g + 4],
                     rows0_written)
            for b in range(1, NC):
                load_cond(b)
            load(gw_sb[:], gate_w, in_gw)
            load(c1_sb[:], c1, in_gw)
            load(x_sb[:], x.rearrange("(c p) d -> p c d", p=P), in_x)
            sp.wait_ge(spread, 3)
            for e in range(0, E):
                sp.wait_ge(x_turned, e + 2)
                load(v1_sb[:, e], v1[:, e * F:(e + 1) * F], in_v)
                load(v2_sb[:, e].rearrange("p f c -> p (f c)"), v2[:, e * NF * C:(e + 1) * NF * C], in_v)
            groups = sp.value_load(more[0:1, 0:1], min_val=0, max_val=MAX_GROUPS - MIN_GROUPS) + MIN_GROUPS
            sp.wait_ge(scattered, groups * (16 * RING))
            for h in range(2):
                for k in range(K):
                    load(got[:, k, 4 * h:4 * h + 4],
                         picked.rearrange("(k c p) d -> k p c d", p=P, k=K)[k, :, 4 * h:4 * h + 4], got_in[h])
            sp.wait_ge(x1_ready, NC)
            load(out.rearrange("(c p) d -> p c d", p=P), x1[:], out_init)
            sp.wait_ge(row_ready, NC)
            sp.wait_ge(sc_ready, 1)
            load(rows1.rearrange("(c p) d -> p c d", p=P), row[:], rows1_written)

        @block.gpsimd
        def _(pool):
            pool.wait_ge(in_rows, 48)
            pool.partition_broadcast(b1_sb[:], b1_row).then_inc(spread, 1)
            pool.partition_broadcast(b2_sb[:], b2_row).then_inc(spread, 1)
            pool.partition_broadcast(c2b_sb[:].rearrange("p e c -> p (e c)"), c2b_row).then_inc(spread, 1)
            pool.wait_ge(idx_ready, 1)
            pool.wait_ge(rows0_written, 32)
            groups = pool.value_load(more[0:1, 0:1], min_val=0, max_val=MAX_GROUPS - MIN_GROUPS) + MIN_GROUPS

            def rows_at(idx, i):
                return bass.IndirectOffsetOnAxis(ap=idx[:, i:i + 1].bitcast(U32), axis=0)

            def gather(b):
                if b >= RING:
                    pool.wait_ge(x_turned, b - RING + 1)
                pool.indirect_dma_start(out=xs[:, b % RING], out_offset=None, in_=rows0,
                                        in_offset=rows_at(gidx, b)).then_inc(gathered[b % RING], 16)

            def scatter(b):
                pool.wait_ge(y_kept, b + 1)
                pool.indirect_dma_start(out=picked, out_offset=rows_at(sidx, b), in_=y0[:, b], in_offset=None,
                                        bounds_check=K * T - 1, oob_is_err=False).then_inc(scattered, 16)

            LAG = 6

            def move_group(g):
                for b in range(RING * g, RING * g + RING):
                    gather(b)
                    if b >= LAG:
                        scatter(b - LAG)

            def move_rest(g):
                def last():
                    for b in range(RING * g - LAG, RING * g):
                        scatter(b)

                if g == MAX_GROUPS:
                    last()
                    return
                with pool.If(groups > g):
                    move_group(g)
                    move_rest(g + 1)
                with pool.Else():
                    last()

            for g in range(MIN_GROUPS):
                move_group(g)
            move_rest(MIN_GROUPS)

            def gather1(e):
                pool.wait_ge(idx1_ready, e + 1)
                for h in range(NH):
                    i = e * NH + h
                    pool.indirect_dma_start(out=xg[:, i], out_offset=None, in_=rows1,
                                            in_offset=rows_at(idx1, i)).then_inc(gathered1[e], 16)

            def add(e):
                pool.wait_ge(y1_kept, e + 1)
                if e:
                    pool.wait_ge(added[e - 1], 16 * NH)
                for h in range(NH):
                    i = e * NH + h
                    pool.indirect_dma_start(out=out, out_offset=rows_at(idx1, i), in_=y1[:, e % 2, h],
                                            in_offset=None, compute_op=ALU.add).then_inc(added[e], 16)

            pool.wait_ge(rows1_written, 16)
            for e in range(AHEAD + 2):
                gather1(e)
            pool.wait_ge(out_init, 16)
            for e in range(E):
                add(e)
                if e + AHEAD + 2 < E:
                    gather1(e + AHEAD + 2)
            pool.wait_ge(added[E - 1], 16 * NH)

        @block.tensor
        def _(pe):
            ident = const("ident")

            def keep_warm(out_bank, n):
                for _ in range(n):
                    pe.matmul(out_bank[:], ones[:], ones[:].unsqueeze(1).to_broadcast([P, 4, P]), start=True, stop=True)

            pe.wait_ge(consts_ready, 1)
            keep_warm(bank[7], 8)
            pe.wait_ge(in_cond, 16 * N_COND)
            for g in range(2):
                pe.matmul(bank[g][:], a_sb[:], xT_sb[:, 512 * g:512 * g + 512], start=True, stop=True).then_inc(lora_h, 1)
            for g in range(2):
                pe.matmul(bank[2 + g][:], wb_sb[:], xT_sb[:, 512 * g:512 * g + 512], start=True, stop=False)
            for g in range(2):
                pe.wait_ge(lora_s, g + 1)
                pe.matmul(bank[2 + g][:], b_sb[:], hs[:, 512 * g:512 * g + 512], start=False, stop=True).then_inc(proj, 1)
            pe.wait_ge(in_const, 16 * N_CONST)
            for c in range(NC):
                if c % 4 == 0:
                    pe.wait_ge(cT_ready, c // 4 + 1)
                mm = pe.matmul(bank[4][:, E * c:E * c + E], cT[:, P * c:P * c + P], rt_sb[:], start=True, stop=True)
            mm.then_inc(logits, 1)
            for c in range(NC):
                mm = pe.transpose(bank[5 + c // 4][:, P * (c % 4):P * (c % 4) + P], cT[:, P * c:P * c + P], ident)
                if c % 4 == 3:
                    mm.then_inc(c_turned, 1)

            def running_counts(out_ap, m, width):
                pe.matmul(out_ap[:, 0:width], tri[:], m[:, 0:width], start=True, stop=True)
                for d in range(1, NC):
                    pe.matmul(out_ap[:, d * width:NC * width], ones[:], m[:, 0:(NC - d) * width],
                              start=(d == 1), stop=False)
                pe.matmul(out_ap[:, width:NC * width], tri[:], m[:, width:NC * width], start=False, stop=True)

            def totals(out_ap, m, width):
                for c in range(NC):
                    mm = pe.matmul(out_ap, ones[:], m[:, c * width:(c + 1) * width], start=(c == 0), stop=(c == NC - 1))
                return mm

            pe.wait_ge(mask_ready, 1)
            m0 = mask[:].rearrange("p c e -> p (c e)")
            running_counts(bank[7][:, 0:NC * E], m0, E)
            totals(bank[0][:, 0:E], m0, E).then_inc(prefix, 1)
            for i in range(K * NC):
                if i % NC == 0:
                    pe.wait_ge(onehots, i // NC + 1)
                mm = pe.matmul(bank[1][:, 0:2 * NBP], slot1h[:, i], blkv[:, i].rearrange("p v b -> p (v b)"),
                               start=(i == 0), stop=(i == K * NC - 1))
            mm.then_inc(slots, 1)

            keep_warm(bank[0], 14)
            pe.wait_ge(bexp_ready, 1)
            groups = pe.value_load(more[0:1, 0:1], min_val=0, max_val=MAX_GROUPS - MIN_GROUPS) + MIN_GROUPS
            pe.wait_ge(in_w1, 16)
            pe.wait_ge(in_w2, 16)

            def turn_x(k, q, n):
                pe.wait_ge(gathered[q], (k - q) * (16 // RING) + 16)
                if n >= 2:
                    pe.wait_ge(xsT_ready, k - 1)
                pe.transpose(bank[q % 2][:, 0:P], xs[:, q], ident).then_inc(x_turned, 1)

            kept_expert = [pe.alloc_register(f"kept_expert_{q}") for q in range(RING)]

            def up(k, q, n):
                e = pe.value_load(bexi[0:1, bass.ds(k, 1)], min_val=0, max_val=E - 1)
                pe.reg_mov(kept_expert[q], e)
                pe.wait_ge(xsT_ready, k + 1)
                if n >= 2:
                    pe.wait_ge(hb_ready, k - 1)
                pe.matmul(bank[2 + q % 2][:], xsT[:, q % 2], w1_sb[:, bass.ds(e * F, F)], start=True,
                          stop=True).then_inc(h_ready, 1)

            def turn_h(k, q, n):
                pe.wait_ge(hb_ready, k + 1)
                if n >= 2:
                    pe.wait_ge(hT_ready, k - 1)
                for f in range(NF):
                    mm = pe.transpose(bank[4 + q % 2][:, P * f:P * f + P], hb[:, q % 2, P * f:P * f + P], ident)
                mm.then_inc(h_turned, 1)

            def down0(k, q, n):
                reg = pe.alloc_register()
                pe.reg_mov(reg, kept_expert[q])
                e = bass.RuntimeValue.of_register_unchecked(reg).with_bounds(min_val=0, max_val=E - 1)
                pe.wait_ge(hT_ready, k + 1)
                if n >= 2:
                    pe.wait_ge(y_kept, k - 1)
                for f in range(NF):
                    mm = pe.matmul(bank[6 + q % 2][:, 0:C], hT[:, q % 2, P * f:P * f + P],
                                   w2_sb[:, bass.ds(e * (NF * C) + f * C, C)], start=(f == 0), stop=(f == NF - 1))
                mm.then_inc(y_ready, 1)

            run_blocks(pe, groups, [(1, up), (0, turn_x), (2, turn_h), (3, down0)])

            pe.wait_ge(scattered, groups * (16 * RING))
            keep_warm(bank[0], 14)
            pe.wait_ge(in_cw, 16 * NC)

            def turn_x1(b):
                pe.wait_ge(x1_ready, b + 1)
                if b >= 2:
                    pe.wait_ge(x1T_ready, b - 1)
                pe.transpose(bank[b % 2][:, 0:P], x1[:, b], ident).then_inc(x1_turned, 1)

            def up_gate(b):
                pe.wait_ge(x1T_ready, b + 1)
                if b >= 2:
                    pe.wait_ge(hid_ready, b - 1)
                for m in range(4):
                    mm = pe.matmul(bank[2 + b % 2][:, P * m:P * m + P], cw_sb[:, b, P * m:P * m + P], x1T[:, b % 2],
                                   start=True, stop=True)
                mm.then_inc(upgate, 1)

            def down1(b):
                pe.wait_ge(hid_ready, b + 1)
                if b >= 2:
                    pe.wait_ge(dT_ready, b - 1)
                for h in range(2):
                    mm = pe.matmul(bank[4 + b % 2][:, 0:P], cw_sb[:, b, WD + P * h:WD + P * h + P],
                                   hid[:, b % 2, h], start=(h == 0), stop=(h == 1))
                mm.then_inc(down, 1)

            def turn_d(b):
                pe.wait_ge(dT_ready, b + 1)
                if b >= 1:
                    pe.wait_ge(row_ready, b)
                pe.transpose(bank[6][:, 0:P], dT[:, P * b:P * b + P], ident).then_inc(d_turned, 1)
                mm = pe.matmul(bank[7][:, E * b:E * b + E], dT[:, P * b:P * b + P], gw_sb[:], start=True, stop=True)
                return mm

            pe.wait_ge(in_gw, 32)
            for b in range(NC + 3):
                if b < NC:
                    turn_x1(b)
                if 0 <= b - 1 < NC:
                    up_gate(b - 1)
                if 0 <= b - 2 < NC:
                    down1(b - 2)
                if 0 <= b - 3 < NC:
                    mm = turn_d(b - 3)
            mm.then_inc(logits1, 1)

            for s in range(STEPS):
                pe.wait_ge(cmp_ready, s + 1)
                for c in range(NC):
                    mm = pe.matmul(bank[0][:, 0:E * NJ], ones[:], cmp_[:, c], start=(c == 0), stop=(c == NC - 1))
                mm.then_inc(counted, 1)

            pe.wait_ge(gteq_ready, 1)
            running_counts(bank[2][:, 0:NC * E], gteq[:, 0], E)
            running_counts(bank[3][:, 0:NC * E], gteq[:, 1], E)
            totals(bank[4][:, 0:E], gteq[:, 0], E).then_inc(prefix1, 1)

            def find_slots(e):
                pe.wait_ge(onehot1, e + 1)
                if e:
                    pe.wait_ge(idx1_ready, e)
                for c in range(NC):
                    mm = pe.matmul(bank[1][:, 0:2 * NH], one1[:, e % 2, c],
                                   hlfv[:, c, e].rearrange("p v h -> p (v h)"), start=(c == 0), stop=(c == NC - 1))
                mm.then_inc(slots1, 1)

            def turn_xg(e):
                pe.wait_ge(gathered1[e], 16 * NH)
                if e >= 1:
                    pe.wait_ge(xgT_ready, e)
                for h in range(NH):
                    mm = pe.transpose(bank[0][:, P * h:P * h + P], xg[:, e * NH + h, 0:C], ident)
                mm.then_inc(xg_turned, 1)

            def up1(e):
                pe.wait_ge(xgT_ready, e + 1)
                for f in range(NF):
                    g = 2 * (e % 2) + f // 2
                    if f % 2 == 0 and e >= 2:
                        pe.wait_ge(h1T_ready, 4 * (e - 2) + 2 * (f // 2) + 2)
                    mm = pe.matmul(bank[2 + g][:, CAP * (f % 2):CAP * (f % 2) + CAP], v1_sb[:, e, P * f:P * f + P],
                                   xgT[:, e % 2], start=True, stop=True)
                    if f % 2 == 1:
                        mm.then_inc(h1_ready, 1)

            def down_e(e):
                pe.wait_ge(h1T_ready, 4 * (e + 1))
                if e >= 2:
                    pe.wait_ge(y1_ready, e - 1)
                for h in range(NH):
                    for f in range(NF):
                        mm = pe.matmul(bank[6 + e % 2][:, C * h:C * h + C], h1T[:, e % 2, f, P * h:P * h + P],
                                       v2_sb[:, e, f], start=(f == 0), stop=(f == NF - 1))
                mm.then_inc(y1_sent, 1)

            pe.wait_ge(in_v, 16 * 2 * E)
            for e in range(AHEAD):
                find_slots(e)
            keep_warm(bank[7], 10)
            turn_xg(0)
            for e in range(E + 1):
                if e < E:
                    up1(e)
                if e + AHEAD < E:
                    find_slots(e + AHEAD)
                if e + 1 < E:
                    turn_xg(e + 1)
                if e >= 1:
                    down_e(e - 1)

        @block.scalar
        def _(act):
            for g in range(2):
                act.wait_ge(proj, g + 1)
                act.activation(cT[:, 512 * g:512 * g + 512], bank[2 + g][:], ACT.Identity, bias=bb_sb[:]).then_inc(cT_ready, 1)
            for g in range(2):
                act.wait_ge(c_turned, g + 1)
                act.activation(c_tok[:, 4 * g:4 * g + 4].rearrange("p c d -> p (c d)"), bank[5 + g][:], ACT.Copy).then_inc(c_tok_ready, 1)
            act.wait_ge(shift_ready, 1)
            act.activation(expd[:], shifted[:], ACT.Exp).then_inc(exp_ready, 1)
            act.activation(den[:], dif2[:], ACT.Exp).then_inc(exp_ready, 1)
            act.activation(scrap[:], bb_sb[:], ACT.Silu)

            def take_x(k, q, n):
                act.wait_ge(x_turned, k + 1)
                if n >= 2:
                    act.wait_ge(h_ready, k - 1)
                act.activation(xsT[:, q % 2], bank[q % 2][:, 0:P], ACT.Copy).then_inc(xsT_ready, 1)

            def take_h(k, q, n):
                act.wait_ge(h_turned, k + 1)
                if n >= 2:
                    act.wait_ge(y_ready, k - 1)
                act.activation(hT[:, q % 2], bank[4 + q % 2][:], ACT.Relu).then_inc(hT_ready, 1)

            act.wait_ge(bexp_ready, 1)
            groups = act.value_load(more[0:1, 0:1], min_val=0, max_val=MAX_GROUPS - MIN_GROUPS) + MIN_GROUPS
            run_blocks(act, groups, [(0, take_x), (2, take_h)])

            def take_x1(b):
                act.wait_ge(x1_turned, b + 1)
                if b >= 2:
                    act.wait_ge(upgate, b - 1)
                act.activation(x1T[:, b % 2], bank[b % 2][:, 0:P], ACT.Copy).then_inc(x1T_ready, 1)

            def silu(b):
                act.wait_ge(upgate, b + 1)
                if b >= 2:
                    act.wait_ge(hid_ready, b - 1)
                for h in range(2):
                    ins = act.activation(su[:, b % 2, h], bank[2 + b % 2][:, P * h:P * h + P], ACT.Silu,
                                         bias=cw_sb[:, b, BU + h:BU + h + 1])
                ins.then_inc(silu_ready, 1)

            def take_d(b):
                act.wait_ge(down, b + 1)
                act.activation(dT[:, P * b:P * b + P], bank[4 + b % 2][:, 0:P], ACT.Identity,
                               bias=cw_sb[:, b, BD:BD + 1]).then_inc(dT_ready, 1)

            def take_row(b):
                act.wait_ge(d_turned, b + 1)
                act.activation(row[:, b, 0:C], bank[6][:, 0:P], ACT.Copy).then_inc(row_ready, 1)

            for b in range(NC + 3):
                if b < NC:
                    take_x1(b)
                if 0 <= b - 1 < NC:
                    silu(b - 1)
                if 0 <= b - 2 < NC:
                    take_d(b - 2)
                if 0 <= b - 3 < NC:
                    take_row(b - 3)
            act.wait_ge(logits1, 1)
            act.activation(th[:].rearrange("p c e -> p (c e)"), bank[7][:, 0:NC * E], ACT.Tanh, scale=0.5).then_inc(tanh_ready, 1)
            act.activation(scrap[:], bb_sb[:], ACT.Gelu)

            def take_xg(e):
                act.wait_ge(xg_turned, e + 1)
                if e >= 2:
                    act.wait_ge(h1_ready, 2 * (e - 1))
                act.activation(xgT[:, e % 2], bank[0][:, 0:CAP], ACT.Copy).then_inc(xgT_ready, 1)

            def gelu(e):
                if e >= 2:
                    act.wait_ge(y1_sent, e - 1)
                for f in range(NF):
                    if f % 2 == 0:
                        act.wait_ge(h1_ready, 2 * e + f // 2 + 1)
                    act.activation(h1T[:, e % 2, f], bank[2 + 2 * (e % 2) + f // 2][:, CAP * (f % 2):CAP * (f % 2) + CAP],
                                   ACT.Gelu, bias=c1_sb[:, e * NF + f:e * NF + f + 1]).then_inc(h1T_ready, 1)

            take_xg(0)
            for e in range(E):
                gelu(e)
                if e + 1 < E:
                    take_xg(e + 1)

        @block.vector
        def _(v):
            done = [0]

            def link(ins):
                done[0] = done[0] + 1
                ins.then_inc(dve, 1)
                v.wait_ge(dve, done[0])

            def bc(ap, dim, n):
                return ap.unsqueeze(dim).to_broadcast([*ap.shape[:dim], n, *ap.shape[dim:]])

            def int_sum(out_ap, in_ap):
                with nc.allow_low_precision(reason="integers, exact in float32"):
                    return v.tensor_reduce(out_ap, in_ap, AX.X, ALU.add)

            v.memset(ones[:], 1.0).then_inc(consts_ready, 1)
            v.wait_ge(in_cond, 16 * N_COND)
            link(v.tensor_scalar(cr2[:], cr_sb[:], LORA_SCALE, None, ALU.mult))
            for g in range(2):
                v.wait_ge(lora_h, g + 1)
                v.tensor_tensor(hs[:, 512 * g:512 * g + 512].rearrange("p (c t) -> p c t", t=P),
                                bank[g][:].rearrange("p (c t) -> p c t", t=P),
                                bc(cr2[:, 4 * g:4 * g + 4], 2, P), ALU.mult).then_inc(lora_s, 1)
            v.wait_ge(in_const, 16 * N_CONST)
            v.tensor_copy(tri[:], const("tri"))
            link(v.tensor_copy(iota[:], const("iota")))

            link(v.tensor_reduce(cmax[:], crow[:], AX.X, ALU.max))
            link(v.tensor_tensor(carg[:], crow[:], bc(cmax[:], 2, E), ALU.is_equal))
            link(v.tensor_tensor(carg[:], carg[:], bc(const("rev")[0:1], 1, NC), ALU.mult))
            link(v.tensor_reduce(cmax[:], carg[:], AX.X, ALU.max))
            v.tensor_scalar(cexp[:], cmax[:], -1.0, float(E), ALU.mult, ALU.add).then_inc(cexp_ready, 1)

            v.wait_ge(logits, 1)
            link(v.tensor_copy(lg[:].rearrange("p c e -> p (c e)"), bank[4][:, 0:NC * E]))
            for k in range(K):
                src = (lg, lg2)[k]
                link(v.tensor_reduce(top[:, k], src[:], AX.X, ALU.max))
                link(v.tensor_tensor(eq[:], src[:], bc(top[:, k], 2, E), ALU.is_equal))
                link(v.tensor_tensor(eq[:], eq[:], bc(const("rev"), 1, NC), ALU.mult))
                link(v.tensor_reduce(mr[:], eq[:], AX.X, ALU.max))
                link(v.tensor_tensor(sel[:, k], eq[:], bc(mr[:], 2, E), ALU.is_equal))
                if k == 0:
                    link(v.scalar_tensor_tensor(lg2[:], sel[:, 0], NEG, lg[:], ALU.mult, ALU.add))
            v.tensor_tensor(mask[:], sel[:, 0], sel[:, 1], ALU.add).then_inc(mask_ready, 1)
            v.tensor_tensor(dif2[:], top[:, 1], top[:, 0], ALU.subtract)
            v.tensor_tensor(shifted[:], lg[:], bc(top[:, 0], 2, E), ALU.subtract).then_inc(shift_ready, 1)

            v.wait_ge(prefix, 1)
            link(v.tensor_tensor(nbig[:], bc(bank[0][:, 0:E], 2, E), bc(const("blk0"), 1, E), ALU.is_gt))
            link(v.tensor_reduce(nblk[:], nbig[:], AX.X, ALU.add))
            link(v.tensor_tensor(before[:], bc(nblk[:], 1, E), const("lt").rearrange("p (a b) -> p a b", b=E), ALU.mult))
            link(v.tensor_reduce(cblk[:], before[:], AX.X, ALU.add))
            v.tensor_scalar(base[:], cblk[:], float(P), None, ALU.mult)
            link(v.tensor_tensor(cinc[:], cblk[:], nblk[:], ALU.add))
            link(v.tensor_tensor(pos[:], bank[7][:, 0:NC * E].rearrange("p (c e) -> p c e", e=E), bc(base[:], 1, NC), ALU.add))
            for k in range(K):
                ins = v.tensor_tensor(psel[:, k], sel[:, k], pos[:], ALU.mult)
            link(ins)
            link(int_sum(posk[:], psel[:].rearrange("p k c e -> p (k c) e")))
            v.tensor_scalar(blk[:], posk[:], 7, None, ALU.logical_shift_right)
            link(v.tensor_scalar(loc[:], posk[:], P - 1, None, ALU.bitwise_and))
            link(v.tensor_tensor(blk1h[:], bc(iota[:, 0:NBP], 1, K * NC), bc(blk[:], 2, NBP), ALU.is_equal))
            v.tensor_scalar(blkv[:, :, 0], blk1h[:], const("pcol"), None, ALU.mult)
            v.tensor_tensor(blkv[:, :, 1], blk1h[:], bc(const("dval"), 2, NBP), ALU.mult)
            for i in range(K * NC):
                ins = v.tensor_scalar(slot1h[:, i], iota[:], loc[:, i:i + 1], None, ALU.is_equal)
                if i % NC == NC - 1:
                    ins.then_inc(onehots, 1)
            link(v.tensor_tensor(bexp[:], bc(cinc[0:1], 1, NBP), bc(iota[0:1, 0:NBP], 2, E), ALU.is_le))
            link(v.tensor_reduce(bexf[:], bexp[:], AX.X, ALU.add))
            link(v.tensor_scalar(nall[:], cinc[0:1, E - 1:E], float(RING - 1 - RING * MIN_GROUPS), None, ALU.add))
            link(v.tensor_scalar(more[:], nall[:], 2, None, ALU.logical_shift_right))
            v.tensor_scalar(bexi[:], bexf[:], float(E - 1), None, ALU.min).then_inc(bexp_ready, 1)
            v.wait_ge(slots, 1)
            link(v.tensor_reduce(idxf[:], bank[1][:, 0:2 * NBP].rearrange("p (v b) -> p b v", v=2), AX.X, ALU.add))
            link(v.tensor_scalar(sidx[:], idxf[:], float(PAD), None, ALU.add))
            v.tensor_scalar(gidx[:], sidx[:], T - 1, None, ALU.bitwise_and).then_inc(idx_ready, 1)

            v.wait_ge(spread, 3)

            def add_b1(k, q, n):
                e = v.value_load(bexi[0:1, bass.ds(k, 1)], min_val=0, max_val=E - 1)
                v.wait_ge(h_ready, k + 1)
                if n >= 2:
                    v.wait_ge(h_turned, k - 1)
                v.tensor_tensor(hb[:, q % 2], bank[2 + q % 2][:], b1_sb[:, bass.ds(e * F, F)], ALU.add).then_inc(hb_ready, 1)

            def add_b2(k, q, n):
                e = v.value_load(bexi[0:1, bass.ds(k, 1)], min_val=0, max_val=E - 1)
                v.wait_ge(y_ready, k + 1)
                v.tensor_tensor(y0[:, bass.ds(k, 1)].rearrange("p o c -> p (o c)"), bank[6 + q % 2][:, 0:C],
                                b2_sb[:, bass.ds(e * C, C)], ALU.add).then_inc(y_kept, 1)

            v.wait_ge(bexp_ready, 1)
            groups = v.value_load(more[0:1, 0:1], min_val=0, max_val=MAX_GROUPS - MIN_GROUPS) + MIN_GROUPS
            run_blocks(v, groups, [(1, add_b1), (3, add_b2)])

            v.wait_ge(exp_ready, 2)
            link(v.tensor_reduce(zsum[:], expd[:], AX.X, ALU.add))
            link(v.scalar_tensor_tensor(den2[:], zsum[:], 1e-9, den[:], ALU.mult, ALU.add))
            link(v.tensor_scalar(den2[:], den2[:], 1.0, None, ALU.add))
            link(v.reciprocal(wt[:, 0], den2[:]))
            link(v.tensor_tensor(wt[:, 1], wt[:, 0], den[:], ALU.mult))
            v.wait_ge(in_x, 16)

            def add_first(c):
                v.wait_ge(got_in[c // 4], 32)
                v.scalar_tensor_tensor(xa[:, c], got[:, 0, c], wt[:, 0, c:c + 1], x_sb[:, c], ALU.mult, ALU.add).then_inc(xa_ready, 1)

            add_first(0)
            for c in range(NC):
                if c + 1 < NC:
                    add_first(c + 1)
                v.wait_ge(xa_ready, c + 1)
                v.scalar_tensor_tensor(x1[:, c], got[:, 1, c], wt[:, 1, c:c + 1], xa[:, c], ALU.mult, ALU.add).then_inc(x1_ready, 1)

            v.wait_ge(in_cw, 16 * NC)
            for b in range(NC):
                v.wait_ge(silu_ready, b + 1)
                if b >= 2:
                    v.wait_ge(down, b - 1)
                for h in range(2):
                    ins = v.scalar_tensor_tensor(hid[:, b % 2, h], bank[2 + b % 2][:, P * (2 + h):P * (3 + h)],
                                                 cw_sb[:, b, BG + h:BG + h + 1], su[:, b % 2, h], ALU.add, ALU.mult)
                ins.then_inc(hid_ready, 1)

            v.wait_ge(tanh_ready, 1)
            link(v.tensor_scalar(sc[:], th[:], 1.0, 0.5, ALU.add, ALU.mult))
            v.tensor_copy(row[:, :, C:ROW], sc[:]).then_inc(sc_ready, 1)

            link(v.memset(tau[:], 0.0))
            for s in range(STEPS):
                digit = const("digits")[:, NJ * s:NJ * s + NJ]
                link(v.tensor_tensor(thr[:], bc(tau[:], 1, NJ), bc(digit, 2, E), ALU.add))
                v.tensor_tensor(cmp_[:].rearrange("p c (j e) -> p c j e", j=NJ), bc(sc[:], 2, NJ),
                                bc(thr[:], 1, NC), ALU.is_ge).then_inc(cmp_ready, 1)
                v.wait_ge(counted, s + 1)
                link(v.scalar_tensor_tensor(reach[:], bank[0][:, 0:E * NJ].rearrange("p (j e) -> p j e", j=NJ), float(CAP),
                                            thr[:], ALU.is_ge, ALU.mult))
                link(v.tensor_reduce(tau[:], reach[:].rearrange("p j e -> p e j"), AX.X, ALU.max))

            gt = gteq[:, 0].rearrange("p (c e) -> p c e", e=E)
            at = gteq[:, 1].rearrange("p (c e) -> p c e", e=E)
            v.tensor_tensor(gt, sc[:], bc(tau[:], 1, NC), ALU.is_gt)
            ins = v.tensor_tensor(at, sc[:], bc(tau[:], 1, NC), ALU.is_equal)
            ins.then_inc(gteq_ready, 1)
            v.wait_ge(prefix1, 1)
            v.tensor_copy(ngt[:], bank[4][:, 0:E])
            link(v.tensor_tensor(pg_[:], bank[2][:, 0:NC * E].rearrange("p (c e) -> p c e", e=E), gt, ALU.mult))
            link(v.tensor_tensor(pe_[:], bank[3][:, 0:NC * E].rearrange("p (c e) -> p c e", e=E), bc(ngt[:], 1, NC), ALU.add))
            link(v.tensor_tensor(pe_[:], pe_[:], at, ALU.mult))
            link(v.tensor_tensor(pos1[:], pg_[:], pe_[:], ALU.add))
            link(v.tensor_tensor(pg_[:], gt, at, ALU.add))
            link(v.tensor_scalar(pg_[:], pg_[:], -float(T), float(T), ALU.mult, ALU.add))
            link(v.tensor_tensor(posi[:].rearrange("p (c e) -> p c e", e=E), pos1[:], pg_[:], ALU.add))
            v.tensor_scalar(half[:], posi[:], 7, None, ALU.logical_shift_right)
            link(v.tensor_scalar(loc1[:], posi[:], P - 1, None, ALU.bitwise_and))
            link(v.tensor_tensor(hlf1h[:], bc(iota[:, 0:NH], 1, NC * E), bc(half[:], 2, NH), ALU.is_equal))
            v.tensor_scalar(hlfv[:, :, :, 0].rearrange("p c e h -> p (c e) h"), hlf1h[:], const("pcol"), None, ALU.mult)
            v.tensor_tensor(hlfv[:, :, :, 1].rearrange("p c e h -> p c e h"), hlf1h[:].rearrange("p (c e) h -> p c e h", e=E),
                            bc(bc(const("cval"), 2, E), 3, NH), ALU.mult)
            def place(e):
                if e >= 2:
                    v.wait_ge(slots1, e - 1)
                for c in range(NC):
                    ins = v.tensor_scalar(one1[:, e % 2, c], iota[:], loc1[:, c * E + e:c * E + e + 1], None, ALU.is_equal)
                ins.then_inc(onehot1, 1)

            def index(e):
                v.wait_ge(slots1, e + 1)
                int_sum(idx1[:, NH * e:NH * e + NH],
                        bank[1][:, 0:2 * NH].rearrange("p (v h) -> p h v", v=2)).then_inc(idx1_ready, 1)

            def score(e):
                v.wait_ge(y1_sent, e + 1)
                if e >= 2:
                    v.wait_ge(added[e - 2], 16 * NH)
                v.tensor_tensor(yb[:, e % 2], bank[6 + e % 2][:, 0:NH * C].rearrange("p (h c) -> p h c", c=C),
                                bc(c2b_sb[:, e], 1, NH), ALU.add).then_inc(y1_ready, 1)
                v.wait_ge(y1_ready, e + 1)
                for h in range(NH):
                    ins = v.tensor_scalar(y1[:, e % 2, h], yb[:, e % 2, h], xg[:, e * NH + h, C + e:C + e + 1], None, ALU.mult)
                ins.then_inc(y1_kept, 1)

            for e in range(E + AHEAD + 1):
                if e < E:
                    place(e)
                    index(e)
                if 0 <= e - AHEAD - 1 < E:
                    score(e - AHEAD - 1)


def kernel(x, cond_8, L0_cond_W_base, L0_cond_b_base, L0_cond_As, L0_cond_Bs, L0_ffn_router_w, L0_ffn_w1,
           L0_ffn_b1, L0_ffn_w2, L0_ffn_b2, L1_cond_W_up, L1_cond_b_up, L1_cond_W_gate, L1_cond_b_gate,
           L1_cond_W_down, L1_cond_b_down, L1_ffn_Wg, L1_ffn_W1, L1_ffn_b1, L1_ffn_W2, L1_ffn_b2):
    import concourse.bacc as _bacc
    from concourse.bass_utils import run_bass_kernel_spmd as _run

    a = np.asarray
    table = constants()
    xf = a(x).reshape(T, C)
    parts = (P, E, F // P, C)
    cond_w = np.concatenate([
        a(L1_cond_W_up).transpose(0, 2, 1), a(L1_cond_W_gate).transpose(0, 2, 1),
        a(L1_cond_W_down).transpose(0, 2, 1).reshape(E, 2, P, C).transpose(0, 2, 1, 3).reshape(E, P, 2 * C),
        a(L1_cond_b_up).reshape(E, 2, P).transpose(0, 2, 1), a(L1_cond_b_gate).reshape(E, 2, P).transpose(0, 2, 1),
        a(L1_cond_b_down).reshape(E, P, 1)], axis=2)
    laid_out = {
        "xT": xf.T,
        "x": xf,
        "lora_a": a(L0_cond_As).reshape(E * R, C).T,
        "lora_b": a(L0_cond_Bs).transpose(0, 2, 1).reshape(E * R, C),
        "w_base": a(L0_cond_W_base).T,
        "b_base": a(L0_cond_b_base).reshape(C, 1),
        "cond_rep": np.repeat(a(cond_8).T, R, axis=0),
        "cond_row": a(cond_8).reshape(1, NC * E),
        "router": a(L0_ffn_router_w).T,
        "w1": a(L0_ffn_w1).transpose(2, 0, 1).reshape(C, E * F),
        "b1": a(L0_ffn_b1).reshape(1, E * F),
        "w2": a(L0_ffn_w2).transpose(2, 0, 1).reshape(NF, P, E, C).transpose(1, 2, 0, 3).reshape(P, E * NF * C),
        "b2": a(L0_ffn_b2).reshape(1, E * C),
        "cond_w": cond_w,
        "gate_w": a(L1_ffn_Wg),
        "v1": a(L1_ffn_W1).transpose(1, 0, 2).reshape(C, E * F),
        "c1": a(L1_ffn_b1).reshape(E, NF, P).transpose(2, 0, 1).reshape(P, E * NF),
        "v2": a(L1_ffn_W2).reshape(E, NF, P, C).transpose(2, 0, 1, 3).reshape(P, E * NF * C),
        "c2b": a(L1_ffn_b2).reshape(1, E * C),
        "consts": table,
    }
    nc = _bacc.Bacc("TRN2", target_bir_lowering=False, num_devices=1)
    arrays, args = {}, []
    for name, v in laid_out.items():
        v = np.ascontiguousarray(v)
        arrays[f"in_{name}"] = v
        args.append(nc.dram_tensor(f"in_{name}", v.shape, mybir.dt.from_np(v.dtype), kind="ExternalInput").ap())
    args.append(nc.dram_tensor("out_x", (T, C), F32, kind="ExternalOutput").ap())
    adaln_moe(nc, *args)
    r = _run(nc, [arrays], core_ids=[0])
    return r.results[0]["out_x"].reshape(NC, P, C)
```

```python
from contextlib import ExitStack

import numpy as np

import concourse.bass as bass
from concourse import mybir

P = 128
T, C = 1024, 128
NC = T // P
E = 8
R = 16
F = 512
NF = F // P
FW = F + NF
H = 256
K = 2
LORA_SCALE = 32.0 / R
RING = 4
NB = K * T // P + E - 1
MIN_BLOCKS = K * T // P
MIN_GROUPS = MIN_BLOCKS // RING
MAX_GROUPS = -(-NB // RING)
NBP = MAX_GROUPS * RING
CAP = 256
NH = CAP // P
PAD = 4096
ROW = C + E
NJ = P // E
DIGITS = [float(NJ) ** -(s + 1) for s in range(6)] + [2.0 ** -25]
STEPS = len(DIGITS)
NEG = -3.0e38

F32 = mybir.dt.float32
BF16 = mybir.dt.bfloat16
I32 = mybir.dt.int32
I16 = mybir.dt.int16
U32 = mybir.dt.uint32
ALU = mybir.AluOpType
ACT = mybir.ActivationFunctionType
AX = mybir.AxisListType

_WIDTHS = [("ident", P), ("tri", P), ("iota", P), ("rev", E), ("pcol", 1), ("blk0", E), ("lt", E * E),
           ("dval", K * NC), ("cval", NC), ("same", P), ("steps", STEPS)]
_AT, _n = {}, 0
for _name, _w in _WIDTHS:
    _AT[_name] = (_n, _n + _w)
    _n += _w
CONSTS = _n
BO, RT, CR, WB, LA, BB = 0, P, P + E, P + 2 * E, 2 * P + 2 * E, 3 * P + 2 * E
FIRST = BB + 1
B2R, C2R, CNR = 0, E * C, 2 * E * C
ROWS = CNR + NC * E
WU, WG, WD, BU, BG, BD = 0, H, 2 * H, 3 * H, 3 * H + 2, 3 * H + 4
CW = 3 * H + 5


def constants():
    t = np.zeros((P, CONSTS), np.float32)
    p = np.arange(P)

    def put(name, v):
        a, b = _AT[name]
        t[:, a:b] = v

    put("ident", np.eye(P))
    put("tri", p[:, None] < p[None, :])
    put("iota", p[None, :])
    put("rev", E - np.arange(E)[None, :])
    put("pcol", p[:, None])
    put("blk0", P * np.arange(E)[None, :])
    e = np.arange(E)
    put("lt", (e[None, :] < e[:, None]).reshape(1, -1))
    k, c = np.meshgrid(np.arange(K), np.arange(NC), indexing="ij")
    put("dval", (P * c + T * k - PAD).reshape(1, -1))
    put("cval", P * np.arange(NC)[None, :])
    put("same", p[:, None] // NJ == p[None, :] // NJ)
    put("steps", (p[:, None] % NJ + 1) * np.array(DIGITS)[None, :])
    return t


def adaln_moe(nc, xT, x, first, second, rows, w1, w2, cond_w, gate_w, v1, c1, v2, consts, out):
    with ExitStack() as ctx:
        def sb(name, shape, dt=F32):
            return ctx.enter_context(nc.sbuf_tensor(name, shape, dt))

        def sem(name):
            return ctx.enter_context(nc.semaphore(name))

        rows0 = nc.dram_tensor("rows0", (T, C), F32).ap()
        rows1 = nc.dram_tensor("rows1", (T, ROW), F32).ap()
        picked = nc.dram_tensor("picked", (K * T, C), F32).ap()

        bank = [ctx.enter_context(nc.psum_tensor(f"bank{i}", [P, 512], F32)) for i in range(8)]

        xT_sb = sb("xT_sb", [P, T])
        x_sb = sb("x_sb", [P, NC, C])
        first_sb = sb("first_sb", [P, FIRST])
        bT_sb = first_sb[:, BO:BO + E * R]
        rt_sb = first_sb[:, RT:RT + E]
        cr_sb = first_sb[:, CR:CR + NC]
        wb_sb = first_sb[:, WB:WB + C]
        a_sb = first_sb[:, LA:LA + C]
        bb_sb = first_sb[:, BB:BB + 1]
        b_sb = sb("b_sb", [P, C])
        w1_sb = sb("w1_sb", [P, E * FW])
        w2_sb = sb("w2_sb", [P, E * NF * C])
        b2_sb = sb("b2_sb", [P, E * C])
        cw_sb = sb("cw_sb", [P, NC, CW])
        gw_sb = sb("gw_sb", [P, P])
        v1_sb = sb("v1_sb", [P, E, F])
        c1_sb = sb("c1_sb", [P, E * NF])
        v2_sb = sb("v2_sb", [P, E, NF, C])
        c2b_sb = sb("c2b_sb", [P, E, C])
        cst = sb("cst", [P, CONSTS])
        rows_in = v2_sb[0:1].rearrange("p e f c -> p (e f c)")[:, 0:ROWS]
        b2_row = rows_in[:, B2R:B2R + E * C]
        c2b_row = rows_in[:, C2R:C2R + E * C]
        crow = rows_in[:, CNR:CNR + NC * E].rearrange("p (b e) -> p b e", e=E)

        def const(name):
            a, b = _AT[name]
            return cst[:, a:b]

        tri = sb("tri", [P, P], BF16)
        iota = sb("iota", [P, P], BF16)
        ones = sb("ones", [P, P], BF16)
        same = sb("same", [P, P], BF16)

        cr2 = sb("cr2", [P, NC])
        m1s = sb("m1s", [P, NC, E])
        gmat = sb("gmat", [P, 2, NC, E])
        bsc = sb("bsc", [P, T])
        w_eff = sb("w_eff", [P, T])
        c_tok = sb("c_tok", [P, NC, C])
        lg = sb("lg", [P, NC, E])
        lg2 = sb("lg2", [P, NC, E])
        eq = sb("eq", [P, NC, E])
        top = sb("top", [P, K, NC])
        mr = sb("mr", [P, NC])
        sel = sb("sel", [P, K, NC, E])
        mask = sb("mask", [P, NC, E], BF16)
        nbig = sb("nbig", [P, E, E])
        nblk = sb("nblk", [P, E])
        before = sb("before", [P, E, E])
        cblk = sb("cblk", [P, E])
        cinc = sb("cinc", [P, E])
        base = sb("base", [P, E])
        pos = sb("pos", [P, NC, E])
        psel = sb("psel", [P, K, NC, E])
        posk = sb("posk", [P, K * NC], I16)
        blk = sb("blk", [P, K * NC], I16)
        loc = sb("loc", [P, K * NC], I16)
        slot1h = sb("slot1h", [P, P, K * NC], BF16)
        blk1h = sb("blk1h", [P, K * NC, NBP], BF16)
        blkv = sb("blkv", [P, K * NC, 2, NBP], BF16)
        idxf = sb("idxf", [P, NBP])
        sidx = sb("sidx", [P, NBP], I32)
        gidx = sb("gidx", [P, NBP], I32)
        bexp = sb("bexp", [1, NBP, E])
        bexf = sb("bexf", [1, NBP])
        bexi = sb("bexi", [1, NBP], I32)
        nall = sb("nall", [1, 1], I32)
        extra = sb("extra", [1, 1], I32)
        more = sb("more", [1, 1], I32)
        shifted = sb("shifted", [P, NC, E])
        expd = sb("expd", [P, NC, E])
        zsum = sb("zsum", [P, NC])
        dif2 = sb("dif2", [P, NC])
        scrap = sb("scrap", [P, 1])
        wt = sb("wt", [P, K, NC])
        den = sb("den", [P, NC])
        den2 = sb("den2", [P, NC])

        xs = sb("xs", [P, RING, C])
        xsT = sb("xsT", [P, 2, P])
        w1_now = sb("w1_now", [P, 2, FW])
        hT = sb("hT", [P, 2, F])
        y0 = sb("y0", [P, NBP, C])
        got = sb("got", [P, K, NC, C])
        xa = bsc[:].rearrange("p (c d) -> p c d", c=NC)
        cols0 = y0[:, 0:NC].rearrange("p c d -> p (c d)").bitcast(BF16).rearrange("p (s i) -> p s i", i=K * NC)
        cols1 = xT_sb[:].bitcast(BF16).rearrange("p (s i) -> p s i", i=K * NC)
        x1 = c_tok

        carg = sb("carg", [1, NC, E])
        cmax = sb("cmax", [1, NC])
        cexp = sb("cexp", [1, NC], I32)
        x1T = sb("x1T", [P, 2, P])
        su = sb("su", [P, 2, 2, P])
        hid = sb("hid", [P, 2, 2, P])
        dT = w_eff
        row = sb("row", [P, NC, ROW])
        sc = sb("sc", [P, NC, E])
        th = got[:, 0].rearrange("p c d -> p (c d)")
        scT = got[:, 1].rearrange("p c d -> p (c d)")
        reached = bsc[:].bitcast(BF16)[:, 0:T]
        count = sb("count", [P, 1])
        enough = sb("enough", [P, 1], BF16)
        tau = sb("tau", [P, 1])
        thr = sb("thr", [P, 1])
        ahead = sb("ahead", [P, 1])
        gteq = sb("gteq", [P, 2, NC * E], BF16)
        pe_ = sb("pe_", [P, NC, E])
        pg_ = sb("pg_", [P, NC, E])
        past = sb("past", [P, NC, E])
        posi = sb("posi", [P, NC * E], I16)
        half = sb("half", [P, NC * E], I16)
        loc1 = sb("loc1", [P, E, NC], I16)
        one1 = slot1h[:].rearrange("p s i -> p (s i)").rearrange("p (r s c) -> p r s c", r=2, c=NC)
        hlf1h = sb("hlf1h", [P, NC * E, NH], BF16)
        hlfv = sb("hlfv", [P, NC, E, 2, NH], BF16)
        idx1 = sb("idx1", [P, E * NH], I32)
        xg = sb("xg", [P, E * NH, ROW])
        xgT = sb("xgT", [P, 2, CAP])
        h1T = sb("h1T", [P, 2, NF, CAP])
        yb = sb("yb", [P, 2, NH, C])
        y1 = sb("y1", [P, 2, NH, C])

        in_first, in_xT, in_const, in_second, in_w1, in_w2, in_x, in_cw = (sem(n) for n in (
            "in_first", "in_xT", "in_const", "in_second", "in_w1", "in_w2", "in_x", "in_cw"))
        in_gw, in_v, in_rows, spread = sem("in_gw"), sem("in_v"), sem("in_rows"), sem("spread")
        dve = sem("dve_steps")
        consts_ready = sem("consts_ready")
        cexp_ready = sem("cexp_ready")
        cr2_ready, m1_ready, m1s_ready, g_ready, gmat_ready, logits = (sem(n) for n in (
            "cr2_ready", "m1_ready", "m1s_ready", "g_ready", "gmat_ready", "logits"))
        bsc_ready, w_summed, w_eff_ready, cols_ready = (sem(n) for n in (
            "bsc_ready", "w_summed", "w_eff_ready", "cols_ready"))
        hlf1h_ready, hlfv_ready = sem("hlf1h_ready"), [sem("hlfv_ready_0"), sem("hlfv_ready_1")]
        blk1h_ready, blkv_ready = sem("blk1h_ready"), [sem("blkv_ready_0"), sem("blkv_ready_1")]
        projected, c_tok_ready, rows0_written = sem("projected"), sem("c_tok_ready"), sem("rows0_written")
        mask_ready, prefix, onehots, slots = (sem(n) for n in ("mask_ready", "prefix", "onehots", "slots"))
        idx_ready, bexp_ready, shift_ready, exp_ready = (sem(n) for n in (
            "idx_ready", "bexp_ready", "shift_ready", "exp_ready"))
        gathered = [sem(f"gathered_{q}") for q in range(RING)]
        x_turned, xsT_ready, w1_now_ready, h_ready, hT_ready, y_ready, y_kept, scattered, xa_ready = (
            sem(n) for n in ("x_turned", "xsT_ready", "w1_now_ready", "h_ready", "hT_ready",
                             "y_ready", "y_kept", "scattered", "xa_ready"))
        PIECES = [(0, 1), (1, 4), (4, NC)]
        got_in = [sem(f"got_in_{h}") for h in range(len(PIECES))]
        x1_ready, x1_turned, x1T_ready, upgate, silu_ready, hid_ready, down, dT_ready = (sem(n) for n in (
            "x1_ready", "x1_turned", "x1T_ready", "upgate", "silu_ready", "hid_ready", "down", "dT_ready"))
        d_turned, row_ready, logits1, tanh_ready, scT_ready, s_turned, sc_ready, rows1_written, out_init = (sem(n) for n in (
            "d_turned", "row_ready", "logits1", "tanh_ready", "scT_ready", "s_turned", "sc_ready", "rows1_written", "out_init"))
        enough_ready, counted, tau_ready, tau_spread, gteq_ready, prefix1, onehot1, slots1, idx1_ready = (sem(n) for n in (
            "enough_ready", "counted", "tau_ready", "tau_spread", "gteq_ready", "prefix1", "onehot1", "slots1", "idx1_ready"))
        gathered1 = [sem(f"gathered1_{e}") for e in range(E)]
        added = [sem(f"added_{e}") for e in range(E)]
        xg_turned, xgT_ready, h1_ready, h1T_ready, y1_ready, y1_kept, y1_sent = (sem(n) for n in (
            "xg_turned", "xgT_ready", "h1_ready", "h1T_ready", "y1_ready", "y1_kept", "y1_sent"))

        AHEAD = 4
        GATHERS_AHEAD = 5

        def run_blocks(eng, groups, stages):
            def step(k, q, first, last=0):
                for i, work in stages:
                    if first >= i >= last:
                        work(k - i, (q - i) % RING, first - i)

            for k in range(RING):
                step(k, k, k)
            with eng.Fori(1, groups) as g:
                for q in range(RING):
                    step(RING * g + q, q, NBP)
            for j in range(max(i for i, _ in stages)):
                step(groups * RING + j, j, NBP, last=j + 1)

        block = ctx.enter_context(nc.Block())

        @block.sync
        def _(sp):
            def load(dst, src, s):
                sp.dma_start(dst, src).then_inc(s, 16)

            load(first_sb[:], first, in_first)
            load(xT_sb[:], xT, in_xT)
            load(cst[:], consts, in_const)
            load(b_sb[:], second, in_second)
            load(rows_in, rows, in_rows)
            load(w1_sb[:], w1, in_w1)
            W2H = 6 * NF * C
            load(w2_sb[:, 0:W2H], w2[:, 0:W2H], in_w2)
            for g in range(2):
                sp.wait_ge(c_tok_ready, g + 1)
                load(rows0.rearrange("(c p) d -> p c d", p=P)[:, 4 * g:4 * g + 4], c_tok[:, 4 * g:4 * g + 4],
                     rows0_written)
            load(w2_sb[:, W2H:], w2[:, W2H:], in_w2)

            def load_cond(b):
                e = sp.value_load(cexp[0:1, b:b + 1], min_val=0, max_val=E - 1)
                load(cw_sb[:, b], cond_w[bass.ds(e, 1)].rearrange("o p w -> (o p) w"), in_cw)

            load(gw_sb[:], gate_w, in_gw)
            load(c1_sb[:], c1, in_gw)
            sp.wait_ge(cexp_ready, 1)
            sp.wait_ge(spread, 2)
            for e in range(E):
                sp.wait_ge(x_turned, 2 * e + 1)
                load_cond(e)
                sp.wait_ge(x_turned, 2 * e + 2)
                load(v1_sb[:, e], v1[:, e * F:(e + 1) * F], in_v)
                load(v2_sb[:, e].rearrange("p f c -> p (f c)"), v2[:, e * NF * C:(e + 1) * NF * C], in_v)
            load(x_sb[:], x.rearrange("(c p) d -> p c d", p=P), in_x)
            sp.wait_ge(bexp_ready, 1)
            blocks = sp.value_load(extra[0:1, 0:1], min_val=0, max_val=NB - MIN_BLOCKS) + MIN_BLOCKS
            sp.wait_ge(scattered, blocks * 16)
            for h, (c0, c1_) in enumerate(PIECES):
                for k in range(K):
                    load(got[:, k, c0:c1_], picked.rearrange("(k c p) d -> k p c d", p=P, k=K)[k, :, c0:c1_], got_in[h])
            sp.wait_ge(x1_ready, NC)
            load(out.rearrange("(c p) d -> p c d", p=P), x1[:], out_init)
            sp.wait_ge(row_ready, NC)
            sp.wait_ge(sc_ready, 2)
            load(rows1.rearrange("(c p) d -> p c d", p=P), row[:], rows1_written)

        @block.gpsimd
        def _(pool):
            pool.wait_ge(in_rows, 16)
            pool.partition_broadcast(b2_sb[:], b2_row).then_inc(spread, 1)
            pool.partition_broadcast(c2b_sb[:].rearrange("p e c -> p (e c)"), c2b_row).then_inc(spread, 1)
            pool.wait_ge(in_const, 16)
            pool.wait_ge(blk1h_ready, 1)
            pool.tensor_tensor(blkv[:, :, 1], blk1h[:], const("dval").unsqueeze(2).to_broadcast([P, K * NC, NBP]),
                               ALU.mult).then_inc(blkv_ready[1], 1)
            pool.wait_ge(idx_ready, 1)
            pool.wait_ge(rows0_written, 32)

            def rows_at(idx, i):
                return bass.IndirectOffsetOnAxis(ap=idx[:, i:i + 1].bitcast(U32), axis=0)

            def gather(b):
                if b >= RING:
                    pool.wait_ge(x_turned, b - RING + 1)
                pool.indirect_dma_start(out=xs[:, b % RING], out_offset=None, in_=rows0,
                                        in_offset=rows_at(gidx, b)).then_inc(gathered[b % RING], 16)

            def scatter(b):
                pool.wait_ge(y_kept, b + 1)
                pool.indirect_dma_start(out=picked, out_offset=rows_at(sidx, b), in_=y0[:, b], in_offset=None,
                                        bounds_check=K * T - 1, oob_is_err=False).then_inc(scattered, 16)

            LAG = 6

            def move_group(g):
                for b in range(RING * g, RING * g + RING):
                    gather(b)
                    if b >= LAG:
                        scatter(b - LAG)

            def scatter_rest(b, end):
                if b < end:
                    with pool.If(blocks > b):
                        scatter(b)
                        scatter_rest(b + 1, end)

            def move_rest(g):
                def last():
                    for b in range(RING * g - LAG, max(MIN_BLOCKS, RING * (g - 1) + 1)):
                        scatter(b)
                    scatter_rest(max(MIN_BLOCKS, RING * (g - 1) + 1), RING * g)

                if g == MAX_GROUPS:
                    last()
                    return
                with pool.If(blocks > RING * g):
                    move_group(g)
                    move_rest(g + 1)
                with pool.Else():
                    last()

            for g in range(MIN_GROUPS):
                move_group(g)
            pool.wait_ge(bexp_ready, 1)
            blocks = pool.value_load(extra[0:1, 0:1], min_val=0, max_val=NB - MIN_BLOCKS) + MIN_BLOCKS
            move_rest(MIN_GROUPS)

            def gather1(e):
                pool.wait_ge(idx1_ready, e + 1)
                for h in range(NH):
                    i = e * NH + h
                    pool.indirect_dma_start(out=xg[:, i], out_offset=None, in_=rows1,
                                            in_offset=rows_at(idx1, i)).then_inc(gathered1[e], 16)

            def add(e):
                if e:
                    pool.wait_ge(added[e - 1], 16 * NH)
                for h in range(NH):
                    pool.wait_ge(y1_kept, NH * e + h + 1)
                    i = e * NH + h
                    pool.indirect_dma_start(out=out, out_offset=rows_at(idx1, i), in_=y1[:, e % 2, h],
                                            in_offset=None, compute_op=ALU.add).then_inc(added[e], 16)

            pool.wait_ge(hlf1h_ready, 1)
            pool.tensor_tensor(hlfv[:, :, :, 1], hlf1h[:].rearrange("p (c e) h -> p c e h", e=E),
                               const("cval").unsqueeze(2).unsqueeze(3).to_broadcast([P, NC, E, NH]), ALU.mult).then_inc(hlfv_ready[1], 1)
            pool.wait_ge(rows1_written, 16)
            for e in range(GATHERS_AHEAD):
                gather1(e)
            pool.wait_ge(out_init, 16)
            for e in range(E):
                add(e)
                if e + GATHERS_AHEAD < E:
                    gather1(e + GATHERS_AHEAD)
            pool.wait_ge(added[E - 1], 16 * NH)

        @block.tensor
        def _(pe):
            ident = const("ident")

            def keep_warm(out_bank, n):
                for _ in range(n):
                    pe.matmul(out_bank[:], ones[:], ones[:].unsqueeze(1).to_broadcast([P, 4, P]), start=True, stop=True)

            pe.wait_ge(consts_ready, 1)
            keep_warm(bank[7], 6)
            pe.wait_ge(in_first, 16)
            pe.matmul(bank[0][:, 0:E], bT_sb, rt_sb, start=True, stop=True).then_inc(m1_ready, 1)
            keep_warm(bank[7], 1)
            rt_all = rt_sb.unsqueeze(1).to_broadcast([P, NC, E])
            pe.matmul(bank[1][:, 0:NC * E], wb_sb, rt_all, start=True, stop=False)
            pe.wait_ge(m1s_ready, 1)
            pe.matmul(bank[1][:, 0:NC * E], a_sb, m1s[:].rearrange("p b e -> p (b e)"), start=False, stop=True)
            pe.matmul(bank[1][:, NC * E:2 * NC * E], bb_sb.to_broadcast([P, P]), rt_all, start=True, stop=True).then_inc(g_ready, 1)
            keep_warm(bank[7], 3)
            pe.wait_ge(in_xT, 16)
            pe.wait_ge(gmat_ready, 1)
            for c in range(NC):
                mm = pe.matmul(bank[4][:, E * c:E * c + E], xT_sb[:, P * c:P * c + P], gmat[:, 0, c], start=True, stop=True)
            mm.then_inc(logits, 1)
            pe.wait_ge(in_const, 16)
            for g in range(2):
                pe.matmul(bank[2 + g][:], wb_sb, ident.unsqueeze(1).to_broadcast([P, 4, P]), start=True, stop=False)

            def sum_weights(g):
                pe.wait_ge(bsc_ready, 4 * g + 4)
                pe.matmul(bank[2 + g][:], a_sb, bsc[:, 512 * g:512 * g + 512], start=False, stop=True).then_inc(w_summed, 1)

            def project(g):
                pe.wait_ge(w_eff_ready, g + 1)
                for c in range(4 * g, 4 * g + 4):
                    mm = pe.matmul(bank[5 + g][:, P * (c % 4):P * (c % 4) + P], xT_sb[:, P * c:P * c + P],
                                   w_eff[:, P * c:P * c + P], start=True, stop=True)
                mm.then_inc(projected, 1)

            def running_counts(out_ap, m, width):
                pe.matmul(out_ap[:, 0:width], tri[:], m[:, 0:width], start=True, stop=True)
                for d in range(1, NC):
                    pe.matmul(out_ap[:, d * width:NC * width], ones[:], m[:, 0:(NC - d) * width],
                              start=(d == 1), stop=False)
                pe.matmul(out_ap[:, width:NC * width], tri[:], m[:, width:NC * width], start=False, stop=True)

            def totals(out_ap, m, width):
                for c in range(NC):
                    mm = pe.matmul(out_ap, ones[:], m[:, c * width:(c + 1) * width], start=(c == 0), stop=(c == NC - 1))
                return mm

            sum_weights(0)
            sum_weights(1)
            pe.wait_ge(mask_ready, 1)
            m0 = mask[:].rearrange("p c e -> p (c e)")
            running_counts(bank[7][:, 0:NC * E], m0, E)
            totals(bank[0][:, 0:E], m0, E).then_inc(prefix, 1)
            project(0)
            project(1)
            keep_warm(bank[3], 8)
            for blkv_part in blkv_ready:
                pe.wait_ge(blkv_part, 1)
            pe.wait_ge(onehots, 1)
            for i in range(K * NC):
                mm = pe.matmul(bank[1][:, 0:2 * NBP], slot1h[:, :, i], blkv[:, i].rearrange("p v b -> p (v b)"),
                               start=(i == 0), stop=(i == K * NC - 1))
            mm.then_inc(slots, 1)

            keep_warm(bank[0], 12)
            pe.wait_ge(bexp_ready, 1)
            groups = pe.value_load(more[0:1, 0:1], min_val=0, max_val=MAX_GROUPS - MIN_GROUPS) + MIN_GROUPS
            pe.wait_ge(in_w2, 32)

            def turn_x(k, q, n):
                pe.wait_ge(gathered[q], (k - q) * (16 // RING) + 16)
                if n >= 2:
                    pe.wait_ge(xsT_ready, k - 1)
                pe.transpose(bank[q % 2][:, 0:P], xs[:, q], ident).then_inc(x_turned, 1)

            def up(k, q, n):
                pe.wait_ge(w1_now_ready, k + 1)
                pe.wait_ge(xsT_ready, k + 1)
                if n >= 2:
                    pe.wait_ge(hT_ready, k - 1)
                for f in range(NF):
                    mm = pe.matmul(bank[2 + q % 2][:, P * f:P * f + P], w1_now[:, q % 2, P * f:P * f + P], xsT[:, q % 2],
                                   start=True, stop=True)
                mm.then_inc(h_ready, 1)

            def down0(k, q, n):
                e = pe.value_load(bexi[0:1, bass.ds(k, 1)], min_val=0, max_val=E - 1)
                pe.wait_ge(hT_ready, k + 1)
                if n >= 2:
                    pe.wait_ge(y_kept, k - 1)
                for f in range(NF):
                    mm = pe.matmul(bank[6 + q % 2][:, 0:C], hT[:, q % 2, P * f:P * f + P],
                                   w2_sb[:, bass.ds(e * (NF * C) + f * C, C)], start=(f == 0), stop=(f == NF - 1))
                mm.then_inc(y_ready, 1)

            run_blocks(pe, groups, [(0, turn_x), (1, up), (2, down0)])

            blocks = pe.value_load(extra[0:1, 0:1], min_val=0, max_val=NB - MIN_BLOCKS) + MIN_BLOCKS
            pe.wait_ge(scattered, blocks * 16)
            keep_warm(bank[0], 12)
            pe.wait_ge(in_cw, 16 * NC)

            def turn_x1(b):
                pe.wait_ge(x1_ready, b + 1)
                if b >= 1:
                    pe.wait_ge(x1T_ready, b)
                pe.transpose(bank[0][:, 0:P], x1[:, b], ident).then_inc(x1_turned, 1)

            def up_gate(b):
                pe.wait_ge(x1T_ready, b + 1)
                if b >= 2:
                    pe.wait_ge(hid_ready, b - 1)
                for m in range(4):
                    mm = pe.matmul(bank[2 + b % 2][:, P * m:P * m + P], cw_sb[:, b, P * m:P * m + P], x1T[:, b % 2],
                                   start=True, stop=True)
                mm.then_inc(upgate, 1)

            def down1(b):
                pe.wait_ge(hid_ready, b + 1)
                if b >= 2:
                    pe.wait_ge(dT_ready, b - 1)
                for h in range(2):
                    mm = pe.matmul(bank[4 + b % 2][:, 0:P], cw_sb[:, b, WD + P * h:WD + P * h + P],
                                   hid[:, b % 2, h], start=(h == 0), stop=(h == 1))
                mm.then_inc(down, 1)

            def turn_d(b):
                pe.wait_ge(dT_ready, b + 1)
                if b >= 1:
                    pe.wait_ge(row_ready, b)
                pe.transpose(bank[6][:, 0:P], dT[:, P * b:P * b + P], ident).then_inc(d_turned, 1)
                mm = pe.matmul(bank[(7, 1)[b // 4]][:, P * (b % 4):P * (b % 4) + P], gw_sb[:], dT[:, P * b:P * b + P],
                               start=True, stop=True)
                if b % 4 == 3:
                    mm.then_inc(logits1, 1)

            pe.wait_ge(in_gw, 32)
            for b in range(NC + 3):
                if b < NC:
                    turn_x1(b)
                if 0 <= b - 1 < NC:
                    up_gate(b - 1)
                if 0 <= b - 2 < NC:
                    down1(b - 2)
                if 0 <= b - 3 < NC:
                    turn_d(b - 3)

            for c in range(NC):
                if c % 4 == 0:
                    pe.wait_ge(scT_ready, c // 4 + 1)
                mm = pe.transpose(bank[2 + c // 4][:, P * (c % 4):P * (c % 4) + P], scT[:, P * c:P * c + P], ident)
                if c % 4 == 3:
                    mm.then_inc(s_turned, 1)
            for s in range(STEPS):
                pe.wait_ge(enough_ready, s + 1)
                pe.matmul(bank[4][:, 0:1], same[:], enough[:], start=True, stop=True).then_inc(counted, 1)
            pe.wait_ge(tau_ready, 1)
            pe.transpose(bank[5][:, 0:P], tau[:].to_broadcast([P, P]), ident).then_inc(tau_spread, 1)

            pe.wait_ge(gteq_ready, 1)
            running_counts(bank[2][:, 0:NC * E], gteq[:, 0], E)
            for d in range(NC):
                pe.matmul(bank[3][:, 0:NC * E], ones[:], gteq[:, 0, d * E:(d + 1) * E].unsqueeze(1).to_broadcast([P, NC, E]),
                          start=(d == 0), stop=False)
            for d in range(1, NC):
                pe.matmul(bank[3][:, d * E:NC * E], ones[:], gteq[:, 1, 0:(NC - d) * E], start=False, stop=False)
            pe.matmul(bank[3][:, 0:NC * E], tri[:], gteq[:, 1], start=False, stop=True).then_inc(prefix1, 1)

            def find_slots(e):
                pe.wait_ge(onehot1, e + 1)
                if e:
                    pe.wait_ge(idx1_ready, e)
                for c in range(NC):
                    mm = pe.matmul(bank[1][:, 0:2 * NH], one1[:, e % 2, :, c],
                                   hlfv[:, c, e].rearrange("p v h -> p (v h)"), start=(c == 0), stop=(c == NC - 1))
                mm.then_inc(slots1, 1)

            def turn_xg(e):
                pe.wait_ge(gathered1[e], 16 * NH)
                if e >= 1:
                    pe.wait_ge(xgT_ready, e)
                for h in range(NH):
                    mm = pe.transpose(bank[0][:, P * h:P * h + P], xg[:, e * NH + h, 0:C], ident)
                mm.then_inc(xg_turned, 1)

            def up1(e, h):
                pe.wait_ge(xgT_ready, e + 1)
                g = 2 * (e % 2) + h
                if e >= 2:
                    pe.wait_ge(h1T_ready, 4 * (e - 2) + 2 * h + 2)
                for f in range(2):
                    fc = 2 * h + f
                    mm = pe.matmul(bank[2 + g][:, CAP * f:CAP * f + CAP], v1_sb[:, e, P * fc:P * fc + P],
                                   xgT[:, e % 2], start=True, stop=True)
                mm.then_inc(h1_ready, 1)

            def down_e(e):
                pe.wait_ge(h1T_ready, 4 * (e + 1))
                for h in range(NH):
                    if e >= 1:
                        pe.wait_ge(y1_ready, NH * (e - 1) + h + 1)
                    for f in range(NF):
                        mm = pe.matmul(bank[6 + h][:, 0:C], h1T[:, e % 2, f, P * h:P * h + P],
                                       v2_sb[:, e, f], start=(f == 0), stop=(f == NF - 1))
                    mm.then_inc(y1_sent, 1)

            pe.wait_ge(in_v, 16 * 2 * E)
            keep_warm(bank[7], 6)
            for hlfv_part in hlfv_ready:
                pe.wait_ge(hlfv_part, 1)
            for e in range(AHEAD):
                find_slots(e)
                keep_warm(bank[7], 3)
            turn_xg(0)
            up1(0, 0)
            find_slots(AHEAD)
            up1(0, 1)
            find_slots(AHEAD + 1)
            turn_xg(1)
            find_slots(AHEAD + 2)
            down_e(0)
            up1(1, 0)
            turn_xg(2)
            up1(1, 1)
            find_slots(AHEAD + 3)
            for e in range(2, E):
                if e + 1 < E:
                    turn_xg(e + 1)
                up1(e, 0)
                down_e(e - 1)
                up1(e, 1)
            down_e(E - 1)

        @block.scalar
        def _(act):
            act.wait_ge(in_second, 16)
            act.wait_ge(cr2_ready, 1)
            for c in range(NC):
                act.activation(bsc[:, C * c:C * c + C], b_sb[:], ACT.Identity, scale=cr2[:, c:c + 1]).then_inc(bsc_ready, 1)
            act.wait_ge(in_const, 16)
            act.activation(cols0, const("iota").unsqueeze(2).to_broadcast([P, P, K * NC]), ACT.Copy).then_inc(cols_ready, 1)
            for g in range(2):
                act.wait_ge(w_summed, g + 1)
                act.activation(w_eff[:, 512 * g:512 * g + 512], bank[2 + g][:], ACT.Copy).then_inc(w_eff_ready, 1)
            for g in range(2):
                act.wait_ge(projected, g + 1)
                act.activation(c_tok[:, 4 * g:4 * g + 4].rearrange("p c d -> p (c d)"), bank[5 + g][:], ACT.Copy).then_inc(c_tok_ready, 1)
            act.wait_ge(blk1h_ready, 1)
            act.activation(blkv[:, :, 0], blk1h[:], ACT.Identity, scale=const("pcol")).then_inc(blkv_ready[0], 1)
            act.wait_ge(shift_ready, 1)
            act.activation(expd[:], shifted[:], ACT.Exp).then_inc(exp_ready, 1)
            act.activation(den[:], dif2[:], ACT.Exp).then_inc(exp_ready, 1)
            act.activation(scrap[:], bb_sb, ACT.Silu)
            act.activation(cols1, const("iota").unsqueeze(2).to_broadcast([P, P, K * NC]), ACT.Copy).then_inc(cols_ready, 1)

            def take_x(k, q, n):
                act.wait_ge(x_turned, k + 1)
                if n >= 2:
                    act.wait_ge(h_ready, k - 1)
                act.activation(xsT[:, q % 2], bank[q % 2][:, 0:P], ACT.Identity, bias=bb_sb).then_inc(xsT_ready, 1)

            def take_h(k, q, n):
                act.wait_ge(h_ready, k + 1)
                if n >= 2:
                    act.wait_ge(y_ready, k - 1)
                for f in range(NF):
                    ins = act.activation(hT[:, q % 2, P * f:P * f + P], bank[2 + q % 2][:, P * f:P * f + P], ACT.Relu,
                                         bias=w1_now[:, q % 2, F + f:F + f + 1])
                ins.then_inc(hT_ready, 1)

            act.wait_ge(bexp_ready, 1)
            groups = act.value_load(more[0:1, 0:1], min_val=0, max_val=MAX_GROUPS - MIN_GROUPS) + MIN_GROUPS
            run_blocks(act, groups, [(0, take_x), (1, take_h)])

            def take_x1(b):
                act.wait_ge(x1_turned, b + 1)
                if b >= 2:
                    act.wait_ge(upgate, b - 1)
                act.activation(x1T[:, b % 2], bank[0][:, 0:P], ACT.Copy).then_inc(x1T_ready, 1)

            def silu(b):
                act.wait_ge(upgate, b + 1)
                if b >= 2:
                    act.wait_ge(hid_ready, b - 1)
                for h in range(2):
                    ins = act.activation(su[:, b % 2, h], bank[2 + b % 2][:, P * h:P * h + P], ACT.Silu,
                                         bias=cw_sb[:, b, BU + h:BU + h + 1])
                ins.then_inc(silu_ready, 1)

            def take_d(b):
                act.wait_ge(down, b + 1)
                act.activation(dT[:, P * b:P * b + P], bank[4 + b % 2][:, 0:P], ACT.Identity,
                               bias=cw_sb[:, b, BD:BD + 1]).then_inc(dT_ready, 1)

            def take_row(b):
                act.wait_ge(d_turned, b + 1)
                act.activation(row[:, b, 0:C], bank[6][:, 0:P], ACT.Copy).then_inc(row_ready, 1)

            def squash(g):
                act.wait_ge(logits1, g + 1)
                act.activation(th[:, 512 * g:512 * g + 512], bank[(7, 1)[g]][:], ACT.Tanh, scale=0.5).then_inc(tanh_ready, 1)

            for b in range(NC + 3):
                if b < NC:
                    take_x1(b)
                if 0 <= b - 1 < NC:
                    silu(b - 1)
                if 0 <= b - 2 < NC:
                    take_d(b - 2)
                if 0 <= b - 3 < NC:
                    take_row(b - 3)
                if b == NC - 1:
                    squash(0)
            squash(1)
            for g in range(2):
                act.wait_ge(s_turned, g + 1)
                first_of_each = bank[2 + g][:].rearrange("p (c e j) -> p c e j", c=4, j=NJ)[:, :, :, 0]
                act.activation(sc[:, 4 * g:4 * g + 4], first_of_each, ACT.Copy)
                act.activation(row[:, 4 * g:4 * g + 4, C:ROW], first_of_each, ACT.Copy).then_inc(sc_ready, 1)
            act.activation(scrap[:], bb_sb, ACT.Gelu)
            act.wait_ge(hlf1h_ready, 1)
            act.activation(hlfv[:, :, :, 0].rearrange("p c e h -> p (c e) h"), hlf1h[:], ACT.Identity,
                           scale=const("pcol")).then_inc(hlfv_ready[0], 1)

            def take_xg(e):
                act.wait_ge(xg_turned, e + 1)
                if e >= 2:
                    act.wait_ge(h1_ready, 2 * (e - 1))
                act.activation(xgT[:, e % 2], bank[0][:, 0:CAP], ACT.Copy).then_inc(xgT_ready, 1)

            def gelu(e, h):
                if e >= 2:
                    act.wait_ge(y1_sent, NH * (e - 1))
                act.wait_ge(h1_ready, 2 * e + h + 1)
                for f in range(2):
                    fc = 2 * h + f
                    act.activation(h1T[:, e % 2, fc], bank[2 + 2 * (e % 2) + h][:, CAP * f:CAP * f + CAP],
                                   ACT.Gelu, bias=c1_sb[:, e * NF + fc:e * NF + fc + 1]).then_inc(h1T_ready, 1)

            take_xg(0)
            gelu(0, 0)
            gelu(0, 1)
            take_xg(1)
            gelu(1, 0)
            take_xg(2)
            gelu(1, 1)
            for e in range(2, E):
                if e + 1 < E:
                    take_xg(e + 1)
                for h in range(2):
                    gelu(e, h)

        @block.vector
        def _(v):
            done = [0]

            def link(ins):
                done[0] = done[0] + 1
                ins.then_inc(dve, 1)
                v.wait_ge(dve, done[0])

            def bc(ap, dim, n):
                return ap.unsqueeze(dim).to_broadcast([*ap.shape[:dim], n, *ap.shape[dim:]])

            def int_sum(out_ap, in_ap):
                with nc.allow_low_precision(reason="integers, exact in float32"):
                    return v.tensor_reduce(out_ap, in_ap, AX.X, ALU.add)

            v.memset(ones[:], 1.0).then_inc(consts_ready, 1)
            v.wait_ge(in_first, 16)
            v.tensor_scalar(cr2[:], cr_sb, LORA_SCALE, None, ALU.mult).then_inc(cr2_ready, 1)
            v.wait_ge(cr2_ready, 1)
            v.wait_ge(m1_ready, 1)
            v.tensor_tensor(m1s[:], bc(bank[0][:, 0:E], 1, NC), bc(cr2[:], 2, E), ALU.mult).then_inc(m1s_ready, 1)
            v.wait_ge(g_ready, 1)
            v.tensor_copy(gmat[:].rearrange("p v b e -> p (v b e)"), bank[1][:, 0:2 * NC * E]).then_inc(gmat_ready, 1)
            v.wait_ge(in_const, 16)
            v.tensor_copy(tri[:], const("tri"))
            v.tensor_copy(same[:], const("same"))
            v.memset(tau[:], 0.0)
            v.tensor_copy(iota[:], const("iota"))
            v.wait_ge(gmat_ready, 1)

            v.wait_ge(logits, 1)
            link(v.tensor_tensor(lg[:].rearrange("p c e -> p (c e)"), bank[4][:, 0:NC * E],
                                 gmat[:, 1].rearrange("p c e -> p (c e)"), ALU.add))
            for k in range(K):
                src = (lg, lg2)[k]
                link(v.tensor_reduce(top[:, k], src[:], AX.X, ALU.max))
                link(v.tensor_tensor(eq[:], src[:], bc(top[:, k], 2, E), ALU.is_equal))
                link(v.tensor_tensor(eq[:], eq[:], bc(const("rev"), 1, NC), ALU.mult))
                link(v.tensor_reduce(mr[:], eq[:], AX.X, ALU.max))
                link(v.tensor_tensor(sel[:, k], eq[:], bc(mr[:], 2, E), ALU.is_equal))
                if k == 0:
                    link(v.scalar_tensor_tensor(lg2[:], sel[:, 0], NEG, lg[:], ALU.mult, ALU.add))
            v.tensor_tensor(mask[:], sel[:, 0], sel[:, 1], ALU.add).then_inc(mask_ready, 1)
            v.tensor_tensor(dif2[:], top[:, 1], top[:, 0], ALU.subtract)
            v.tensor_tensor(shifted[:], lg[:], bc(top[:, 0], 2, E), ALU.subtract).then_inc(shift_ready, 1)

            v.wait_ge(prefix, 1)
            link(v.tensor_tensor(nbig[:], bc(bank[0][:, 0:E], 2, E), bc(const("blk0"), 1, E), ALU.is_gt))
            link(v.tensor_reduce(nblk[:], nbig[:], AX.X, ALU.add))
            link(v.tensor_tensor(before[:], bc(nblk[:], 1, E), const("lt").rearrange("p (a b) -> p a b", b=E), ALU.mult))
            link(v.tensor_reduce(cblk[:], before[:], AX.X, ALU.add))
            link(v.tensor_scalar(base[:], cblk[:], float(P), None, ALU.mult))
            link(v.tensor_tensor(pos[:], bank[7][:, 0:NC * E].rearrange("p (c e) -> p c e", e=E), bc(base[:], 1, NC), ALU.add))
            for k in range(K):
                v.tensor_tensor(psel[:, k], sel[:, k], pos[:], ALU.mult)
            link(v.tensor_tensor(cinc[:], cblk[:], nblk[:], ALU.add))
            link(int_sum(posk[:], psel[:].rearrange("p k c e -> p (k c) e")))
            v.tensor_scalar(blk[:], posk[:], 7, None, ALU.logical_shift_right)
            link(v.tensor_scalar(loc[:], posk[:], P - 1, None, ALU.bitwise_and))
            v.tensor_tensor(blk1h[:], bc(iota[:, 0:NBP], 1, K * NC), bc(blk[:], 2, NBP), ALU.is_equal).then_inc(blk1h_ready, 1)
            v.wait_ge(cols_ready, 1)
            v.tensor_tensor(slot1h[:], cols0, bc(loc[:], 1, P), ALU.is_equal).then_inc(onehots, 1)
            link(v.tensor_tensor(bexp[:], bc(cinc[0:1], 1, NBP), bc(iota[0:1, 0:NBP], 2, E), ALU.is_le))
            v.tensor_reduce(bexf[:], bexp[:], AX.X, ALU.add)
            v.tensor_scalar(nall[:], cinc[0:1, E - 1:E], float(RING - 1 - RING * MIN_GROUPS), None, ALU.add)
            v.wait_ge(slots, 1)
            link(v.tensor_reduce(idxf[:], bank[1][:, 0:2 * NBP].rearrange("p (v b) -> p b v", v=2), AX.X, ALU.add))
            link(v.tensor_scalar(sidx[:], idxf[:], float(PAD), None, ALU.add))
            v.tensor_scalar(gidx[:], sidx[:], T - 1, None, ALU.bitwise_and).then_inc(idx_ready, 1)
            v.tensor_scalar(more[:], nall[:], 2, None, ALU.logical_shift_right)
            v.tensor_scalar(extra[:], cinc[0:1, E - 1:E], float(-MIN_BLOCKS), None, ALU.add)
            v.tensor_scalar(bexi[:], bexf[:], float(E - 1), None, ALU.min).then_inc(bexp_ready, 1)

            v.wait_ge(in_rows, 16)
            link(v.tensor_reduce(cmax[:], crow, AX.X, ALU.max))
            link(v.tensor_tensor(carg[:], crow, bc(cmax[:], 2, E), ALU.is_equal))
            link(v.tensor_tensor(carg[:], carg[:], bc(const("rev")[0:1], 1, NC), ALU.mult))
            link(v.tensor_reduce(cmax[:], carg[:], AX.X, ALU.max))
            v.tensor_scalar(cexp[:], cmax[:], -1.0, float(E), ALU.mult, ALU.add).then_inc(cexp_ready, 1)

            v.wait_ge(spread, 2)
            v.wait_ge(in_w1, 16)

            def take_w1(k, q, n):
                e = v.value_load(bexi[0:1, bass.ds(k, 1)], min_val=0, max_val=E - 1)
                if n >= 2:
                    v.wait_ge(hT_ready, k - 1)
                v.tensor_copy(w1_now[:, q % 2], w1_sb[:, bass.ds(e * FW, FW)]).then_inc(w1_now_ready, 1)

            def add_b2(k, q, n):
                e = v.value_load(bexi[0:1, bass.ds(k, 1)], min_val=0, max_val=E - 1)
                v.wait_ge(y_ready, k + 1)
                v.tensor_tensor(y0[:, bass.ds(k, 1)].rearrange("p o c -> p (o c)"), bank[6 + q % 2][:, 0:C],
                                b2_sb[:, bass.ds(e * C, C)], ALU.add).then_inc(y_kept, 1)

            v.wait_ge(bexp_ready, 1)
            groups = v.value_load(more[0:1, 0:1], min_val=0, max_val=MAX_GROUPS - MIN_GROUPS) + MIN_GROUPS
            run_blocks(v, groups, [(0, take_w1), (2, add_b2)])

            v.wait_ge(exp_ready, 2)
            link(v.tensor_reduce(zsum[:], expd[:], AX.X, ALU.add))
            link(v.scalar_tensor_tensor(den2[:], zsum[:], 1e-9, den[:], ALU.mult, ALU.add))
            link(v.tensor_scalar(den2[:], den2[:], 1.0, None, ALU.add))
            link(v.reciprocal(wt[:, 0], den2[:]))
            link(v.tensor_tensor(wt[:, 1], wt[:, 0], den[:], ALU.mult))
            v.wait_ge(in_x, 16)

            def add_first(c):
                for h, (c0, c1_) in enumerate(PIECES):
                    if c == c0:
                        v.wait_ge(got_in[h], 32)
                v.scalar_tensor_tensor(xa[:, c], got[:, 0, c], wt[:, 0, c:c + 1], x_sb[:, c], ALU.mult, ALU.add).then_inc(xa_ready, 1)

            def add_second(c):
                v.wait_ge(xa_ready, c + 1)
                v.scalar_tensor_tensor(x1[:, c], got[:, 1, c], wt[:, 1, c:c + 1], xa[:, c], ALU.mult, ALU.add).then_inc(x1_ready, 1)

            def gate_up(b):
                v.wait_ge(silu_ready, b + 1)
                if b >= 2:
                    v.wait_ge(down, b - 1)
                for h in range(2):
                    ins = v.scalar_tensor_tensor(hid[:, b % 2, h], bank[2 + b % 2][:, P * (2 + h):P * (3 + h)],
                                                 cw_sb[:, b, BG + h:BG + h + 1], su[:, b % 2, h], ALU.add, ALU.mult)
                ins.then_inc(hid_ready, 1)

            v.wait_ge(in_cw, 16 * NC)
            add_first(0)
            add_second(0)
            add_first(1)
            add_second(1)
            add_first(2)
            add_second(2)
            for b in range(NC):
                for c in {0: (3,), 1: (4, 5), 2: (6, 7)}.get(b, ()):
                    add_first(c)
                    add_second(c)
                gate_up(b)

            v.wait_ge(cols_ready, 2)
            for g in range(2):
                v.wait_ge(tanh_ready, g + 1)
                v.tensor_scalar(scT[:, 512 * g:512 * g + 512], th[:, 512 * g:512 * g + 512], 1.0, 0.5, ALU.add,
                                ALU.mult).then_inc(scT_ready, 1)

            v.wait_ge(scT_ready, 2)
            steps = const("steps")
            for s in range(STEPS):
                now = thr[:] if s else steps[:, 0:1]
                link(v.tensor_scalar(reached, scT, now, None, ALU.is_ge, ALU.add, accum_out=count[:]))
                v.tensor_scalar(enough[:], count[:], float(CAP), None, ALU.is_ge).then_inc(enough_ready, 1)
                early = s + 2 < STEPS
                if early:
                    link(v.tensor_tensor(ahead[:], tau[:], steps[:, s + 1:s + 2], ALU.add))
                v.wait_ge(counted, s + 1)
                if early:
                    v.scalar_tensor_tensor(thr[:], bank[4][:, 0:1], DIGITS[s], ahead[:], ALU.mult, ALU.add)
                ins = v.scalar_tensor_tensor(tau[:], bank[4][:, 0:1], DIGITS[s], tau[:], ALU.mult, ALU.add)
                if s + 1 < STEPS:
                    link(ins)
                if s + 2 == STEPS:
                    link(v.tensor_tensor(thr[:], tau[:], steps[:, s + 1:s + 2], ALU.add))
            ins.then_inc(tau_ready, 1)
            v.wait_ge(tau_spread, 1)
            v.wait_ge(sc_ready, 2)
            tau_all = bank[5][:, 0:P].rearrange("p (e j) -> p e j", j=NJ)[:, :, 0]

            gt = gteq[:, 0].rearrange("p (c e) -> p c e", e=E)
            at = gteq[:, 1].rearrange("p (c e) -> p c e", e=E)
            v.tensor_tensor(gt, sc[:], bc(tau_all, 1, NC), ALU.is_gt)
            ins = v.tensor_tensor(at, sc[:], bc(tau_all, 1, NC), ALU.is_equal)
            ins.then_inc(gteq_ready, 1)
            v.wait_ge(gteq_ready, 1)
            link(v.tensor_tensor(pg_[:], gt, at, ALU.add))
            link(v.tensor_scalar(past[:], pg_[:], -float(T), float(T), ALU.mult, ALU.add))
            v.wait_ge(prefix1, 1)
            link(v.tensor_tensor(pg_[:], bank[2][:, 0:NC * E].rearrange("p (c e) -> p c e", e=E), gt, ALU.mult))
            v.tensor_tensor(pg_[:], pg_[:], past[:], ALU.add)
            link(v.tensor_tensor(pe_[:], bank[3][:, 0:NC * E].rearrange("p (c e) -> p c e", e=E), at, ALU.mult))
            link(v.tensor_tensor(posi[:].rearrange("p (c e) -> p c e", e=E), pg_[:], pe_[:], ALU.add))
            v.tensor_scalar(half[:], posi[:], 7, None, ALU.logical_shift_right)
            link(v.tensor_scalar(loc1[:].rearrange("p e c -> p c e"), posi[:].rearrange("p (c e) -> p c e", e=E), P - 1, None,
                                 ALU.bitwise_and))
            v.tensor_tensor(hlf1h[:], bc(iota[:, 0:NH], 1, NC * E), bc(half[:], 2, NH), ALU.is_equal).then_inc(hlf1h_ready, 1)

            def place(e):
                if e >= 2:
                    v.wait_ge(slots1, e - 1)
                v.tensor_tensor(one1[:, e % 2], cols1[:, :, 0:NC], bc(loc1[:, e], 1, P),
                                ALU.is_equal).then_inc(onehot1, 1)

            def index(e):
                v.wait_ge(slots1, e + 1)
                int_sum(idx1[:, NH * e:NH * e + NH],
                        bank[1][:, 0:2 * NH].rearrange("p (v h) -> p h v", v=2)).then_inc(idx1_ready, 1)

            def score(e, h):
                v.wait_ge(y1_sent, NH * e + h + 1)
                if e >= 2:
                    v.wait_ge(added[e - 2], 16 * NH)
                v.tensor_tensor(yb[:, e % 2, h], bank[6 + h][:, 0:C], c2b_sb[:, e], ALU.add).then_inc(y1_ready, 1)
                v.wait_ge(y1_ready, NH * e + h + 1)
                v.tensor_scalar(y1[:, e % 2, h], yb[:, e % 2, h], xg[:, e * NH + h, C + e:C + e + 1], None,
                                ALU.mult).then_inc(y1_kept, 1)

            for e in range(E - 1):
                place(e)
                index(e)
            place(E - 1)
            for e in range(E):
                for h in range(NH):
                    score(e, h)
                if e == 0:
                    index(E - 1)


def kernel(x, cond_8, L0_cond_W_base, L0_cond_b_base, L0_cond_As, L0_cond_Bs, L0_ffn_router_w, L0_ffn_w1,
           L0_ffn_b1, L0_ffn_w2, L0_ffn_b2, L1_cond_W_up, L1_cond_b_up, L1_cond_W_gate, L1_cond_b_gate,
           L1_cond_W_down, L1_cond_b_down, L1_ffn_Wg, L1_ffn_W1, L1_ffn_b1, L1_ffn_W2, L1_ffn_b2):
    import concourse.bacc as _bacc
    from concourse.bass_utils import run_bass_kernel_spmd as _run

    a = np.asarray
    table = constants()
    xf = a(x).reshape(T, C)
    parts = (P, E, F // P, C)
    cond_w = np.concatenate([
        a(L1_cond_W_up).transpose(0, 2, 1), a(L1_cond_W_gate).transpose(0, 2, 1),
        a(L1_cond_W_down).transpose(0, 2, 1).reshape(E, 2, P, C).transpose(0, 2, 1, 3).reshape(E, P, 2 * C),
        a(L1_cond_b_up).reshape(E, 2, P).transpose(0, 2, 1), a(L1_cond_b_gate).reshape(E, 2, P).transpose(0, 2, 1),
        a(L1_cond_b_down).reshape(E, P, 1)], axis=2)
    laid_out = {
        "xT": xf.T,
        "x": xf,
        "first": np.concatenate([
            a(L0_cond_Bs).transpose(1, 0, 2).reshape(C, E * R), a(L0_ffn_router_w).T,
            np.repeat(a(cond_8).T, R, axis=0), a(L0_cond_W_base), a(L0_cond_As).reshape(E * R, C),
            a(L0_cond_b_base).reshape(C, 1)], axis=1),
        "second": a(L0_cond_Bs).transpose(0, 2, 1).reshape(E * R, C),
        "w1": np.concatenate([a(L0_ffn_w1).transpose(2, 0, 1), a(L0_ffn_b1).reshape(E, NF, P).transpose(2, 0, 1)],
                             axis=2).reshape(P, E * FW),
        "rows": np.concatenate([a(L0_ffn_b2).reshape(1, E * C), a(L1_ffn_b2).reshape(1, E * C),
                                a(cond_8).reshape(1, NC * E)], axis=1),
        "w2": a(L0_ffn_w2).transpose(2, 0, 1).reshape(NF, P, E, C).transpose(1, 2, 0, 3).reshape(P, E * NF * C),
        "cond_w": cond_w,
        "gate_w": np.repeat(a(L1_ffn_Wg), NJ, axis=1),
        "v1": a(L1_ffn_W1).transpose(1, 0, 2).reshape(C, E * F),
        "c1": a(L1_ffn_b1).reshape(E, NF, P).transpose(2, 0, 1).reshape(P, E * NF),
        "v2": a(L1_ffn_W2).reshape(E, NF, P, C).transpose(2, 0, 1, 3).reshape(P, E * NF * C),
        "consts": table,
    }
    nc = _bacc.Bacc("TRN2", target_bir_lowering=False, num_devices=1)
    arrays, args = {}, []
    for name in ("xT", "x", "first", "second", "rows", "w1", "w2", "cond_w", "gate_w", "v1", "c1", "v2", "consts"):
        v = np.ascontiguousarray(laid_out[name])
        arrays[f"in_{name}"] = v
        args.append(nc.dram_tensor(f"in_{name}", v.shape, mybir.dt.from_np(v.dtype), kind="ExternalInput").ap())
    args.append(nc.dram_tensor("out_x", (T, C), F32, kind="ExternalOutput").ap())
    adaln_moe(nc, *args)
    r = _run(nc, [arrays], core_ids=[0])
    return r.results[0]["out_x"].reshape(NC, P, C)
```
